# Optimizing a Trainium2 kernel written in Bass

```python
import numpy as np
import jax
import jax.numpy as jnp

def _softmax(x, axis=-1):
    return jax.nn.softmax(x, axis=axis)

def _gelu(x):
    return jax.nn.gelu(x, approximate=True)

def _silu(x):
    return jax.nn.silu(x)

def _sigmoid(x):
    return jax.nn.sigmoid(x)

def _layernorm(x, axis=-1, eps=1e-05):
    m = jnp.mean(x, axis=axis, keepdims=True)
    v = jnp.var(x, axis=axis, keepdims=True)
    return (x - m) / jnp.sqrt(v + eps)

def _scatter_add(tgt, idx, src, axis=0):
    return tgt.at[idx].add(src)

def _segment_sum(src, seg, n):
    return jax.ops.segment_sum(src, seg, n)
kernel_name = 'mk_seq_postln_d1_jaxref_r8_fa68b0'

def setup_inputs(seed: int=0):
    np.random.seed(seed)
    _w = jnp.asarray

    def _L0_attn_setup():
        import jax, jax.numpy as jnp
        import numpy as np
        HIDDEN = 512
        HEAD_DIM = 128
        N_Q_HEADS = 32
        N_KV_HEADS = 8
        SLIDING_WINDOW = 128
        ROPE_THETA = 10000.0
        BATCH, SEQ = (1, 256)

        def _rope(t, pos):
            d = t.shape[-1]
            half = d // 2
            inv_freq = ROPE_THETA ** (-jnp.arange(half, dtype=jnp.float32) / half)
            ang = pos[:, None].astype(jnp.float32) * inv_freq[None, :]
            cos = jnp.cos(ang)[None, :, None, :]
            sin = jnp.sin(ang)[None, :, None, :]
            t1, t2 = (t[..., :half], t[..., half:])
            return jnp.concatenate([t1 * cos - t2 * sin, t1 * sin + t2 * cos], axis=-1)
        key = jax.random.key(seed)
        ks = jax.random.split(key, 5)
        w_scale = HIDDEN ** (-0.5)
        return {'x': jax.random.normal(ks[0], (BATCH, SEQ, HIDDEN), jnp.float32), 'wq': jax.random.normal(ks[1], (HIDDEN, N_Q_HEADS * HEAD_DIM), jnp.float32) * w_scale, 'wk': jax.random.normal(ks[2], (HIDDEN, N_KV_HEADS * HEAD_DIM), jnp.float32) * w_scale, 'wv': jax.random.normal(ks[3], (HIDDEN, N_KV_HEADS * HEAD_DIM), jnp.float32) * w_scale, 'wo': jax.random.normal(ks[4], (N_Q_HEADS * HEAD_DIM, HIDDEN), jnp.float32) * w_scale}
    _L0_attn_in = _L0_attn_setup()

    def _L0_ffn_setup():
        import jax, jax.numpy as jnp
        import numpy as np
        DIM = 512
        HID = 1376
        R = 16
        SCALING = 32.0 / 16.0

        def _lora_linear(x, w, a, b):
            base = jnp.einsum('bsd,od->bso', x, w)
            low = jnp.einsum('bsr,or->bso', jnp.einsum('bsd,rd->bsr', x, a), b)
            return base + low * SCALING
        key = jax.random.key(seed)
        ks = jax.random.split(key, 10)
        s_in = 1.0 / np.sqrt(DIM)
        s_hid = 1.0 / np.sqrt(HID)
        return {'x': jax.random.normal(ks[0], (4, 256, DIM), jnp.float32), 'w1': jax.random.normal(ks[1], (HID, DIM), jnp.float32) * s_in, 'w3': jax.random.normal(ks[2], (HID, DIM), jnp.float32) * s_in, 'w2': jax.random.normal(ks[3], (DIM, HID), jnp.float32) * s_hid, 'lora_A1': jax.random.normal(ks[4], (R, DIM), jnp.float32) * s_in, 'lora_B1': jax.random.normal(ks[5], (HID, R), jnp.float32) * 0.02, 'lora_A3': jax.random.normal(ks[6], (R, DIM), jnp.float32) * s_in, 'lora_B3': jax.random.normal(ks[7], (HID, R), jnp.float32) * 0.02, 'lora_A2': jax.random.normal(ks[8], (R, HID), jnp.float32) * s_hid, 'lora_B2': jax.random.normal(ks[9], (DIM, R), jnp.float32) * 0.02}
    _L0_ffn_in = _L0_ffn_setup()
    _d = {'L0_attn_x': _L0_attn_in['x'], 'L0_attn_wq': _L0_attn_in['wq'], 'L0_attn_wk': _L0_attn_in['wk'], 'L0_attn_wv': _L0_attn_in['wv'], 'L0_attn_wo': _L0_attn_in['wo'], 'L0_ffn_w1': _L0_ffn_in['w1'], 'L0_ffn_w3': _L0_ffn_in['w3'], 'L0_ffn_w2': _L0_ffn_in['w2'], 'L0_ffn_lora_A1': _L0_ffn_in['lora_A1'], 'L0_ffn_lora_B1': _L0_ffn_in['lora_B1'], 'L0_ffn_lora_A3': _L0_ffn_in['lora_A3'], 'L0_ffn_lora_B3': _L0_ffn_in['lora_B3'], 'L0_ffn_lora_A2': _L0_ffn_in['lora_A2'], 'L0_ffn_lora_B2': _L0_ffn_in['lora_B2']}
    _x0 = _d['L0_attn_x']
    _d['L0_attn_x'] = jax.random.normal(jax.random.fold_in(jax.random.key(seed), 1), (2, 1024, 512), dtype=_x0.dtype)
    del _x0
    return _d

def reference(L0_attn_x, L0_attn_wq, L0_attn_wk, L0_attn_wv, L0_attn_wo, L0_ffn_w1, L0_ffn_w3, L0_ffn_w2, L0_ffn_lora_A1, L0_ffn_lora_B1, L0_ffn_lora_A3, L0_ffn_lora_B3, L0_ffn_lora_A2, L0_ffn_lora_B2):

    def _L0_attn_ref(x, wq, wk, wv, wo):
        import jax, jax.numpy as jnp
        import numpy as np
        HIDDEN = 512
        HEAD_DIM = 128
        N_Q_HEADS = 32
        N_KV_HEADS = 8
        SLIDING_WINDOW = 128
        ROPE_THETA = 10000.0
        BATCH, SEQ = (1, 256)

        def _rope(t, pos):
            d = t.shape[-1]
            half = d // 2
            inv_freq = ROPE_THETA ** (-jnp.arange(half, dtype=jnp.float32) / half)
            ang = pos[:, None].astype(jnp.float32) * inv_freq[None, :]
            cos = jnp.cos(ang)[None, :, None, :]
            sin = jnp.sin(ang)[None, :, None, :]
            t1, t2 = (t[..., :half], t[..., half:])
            return jnp.concatenate([t1 * cos - t2 * sin, t1 * sin + t2 * cos], axis=-1)
        B, S, _ = x.shape
        G = N_Q_HEADS // N_KV_HEADS
        sm_scale = HEAD_DIM ** (-0.5)
        q = (x @ wq).reshape(B, S, N_Q_HEADS, HEAD_DIM)
        k = (x @ wk).reshape(B, S, N_KV_HEADS, HEAD_DIM)
        v = (x @ wv).reshape(B, S, N_KV_HEADS, HEAD_DIM)
        pos = jnp.arange(S)
        q = _rope(q, pos)
        k = _rope(k, pos)
        qg = q.reshape(B, S, N_KV_HEADS, G, HEAD_DIM)
        scores = jnp.einsum('bqhgd,bshd->bhgqs', qg, k) * sm_scale
        i = pos[:, None]
        j = pos[None, :]
        allowed = (j <= i) & (j > i - SLIDING_WINDOW)
        neg = jnp.finfo(scores.dtype).min
        scores = jnp.where(allowed[None, None, None], scores, neg)
        attn = jax.nn.softmax(scores, axis=-1)
        out = jnp.einsum('bhgqs,bshd->bqhgd', attn, v).reshape(B, S, N_Q_HEADS * HEAD_DIM)
        return out @ wo

    def _L0_ffn_ref(x, w1, w3, w2, lora_A1, lora_B1, lora_A3, lora_B3, lora_A2, lora_B2):
        import jax, jax.numpy as jnp
        import numpy as np
        DIM = 512
        HID = 1376
        R = 16
        SCALING = 32.0 / 16.0

        def _lora_linear(x, w, a, b):
            base = jnp.einsum('bsd,od->bso', x, w)
            low = jnp.einsum('bsr,or->bso', jnp.einsum('bsd,rd->bsr', x, a), b)
            return base + low * SCALING
        h1 = _lora_linear(x, w1, lora_A1, lora_B1)
        h3 = _lora_linear(x, w3, lora_A3, lora_B3)
        g = jax.nn.silu(h1) * h3
        return _lora_linear(g, w2, lora_A2, lora_B2)
    x = L0_attn_x
    x = _layernorm(x + _L0_attn_ref(x, L0_attn_wq, L0_attn_wk, L0_attn_wv, L0_attn_wo), axis=-1)
    x = _layernorm(x + _L0_ffn_ref(x, L0_ffn_w1, L0_ffn_w3, L0_ffn_w2, L0_ffn_lora_A1, L0_ffn_lora_B1, L0_ffn_lora_A3, L0_ffn_lora_B3, L0_ffn_lora_A2, L0_ffn_lora_B2), axis=-1)
    return x

_drawn_inputs = setup_inputs


def setup_inputs(seed=0):
    import zlib

    import numpy as np

    out = dict(_drawn_inputs(seed))
    spreads = {}
    factors = {}
    for name, (base, spread) in spreads.items():
        noise = np.random.default_rng([zlib.crc32(name.encode()), seed]).standard_normal(out[name].shape)
        drawn = base * np.exp(spread * noise) if base else spread * noise
        out[name] = jnp.asarray(drawn.astype(out[name].dtype))
    for name, factor in factors.items():
        out[name] = (out[name] * factor).astype(out[name].dtype)
    return out
```

```python
from contextlib import ExitStack

import numpy as np
import concourse.bass as bass
from concourse import mybir

BATCH, SEQ, DIM = 2, 1024, 512
HEAD = 128
Q_HEADS, KV_HEADS = 32, 8
GROUP = Q_HEADS // KV_HEADS
THETA = 10000.0
HIDDEN, RANK = 1376, 16
EPS = 1e-5
LORA_SCALE = 2.0

P = 128
KD = DIM // P
CHUNK = 512
BPC = CHUNK // P
BLOCKS = SEQ // P
ALL_BLOCKS = BATCH * BLOCKS
CHUNKS = BATCH * SEQ // CHUNK
ITERS = BATCH * KV_HEADS
PIECES = 10
WO_PIECES = GROUP
PROJ = PIECES - WO_PIECES
K_PROJ, V_PROJ = 4, 5
ROPES = 5
RING = 5
HT = -(-HIDDEN // P)
NEG = float(np.finfo(np.float32).min)

EARLY = [0, 2, K_PROJ, V_PROJ]
LATE = [1, 3, None, None]
SPLITS = {1: [0, 1, 2, 3], 2: [4, 5], 3: [6, 7], 4: [8], 5: [9]}


def attention_and_ffn(nc, x_rows, x_cols, attn_w, rope, later, ident, ffn_w, lora_tile, lora_all, out):
    f32, f32r, i32 = mybir.dt.float32, mybir.dt.float32r, mybir.dt.int32
    ALU, ACT, AX = mybir.AluOpType, mybir.ActivationFunctionType, mybir.AxisListType
    SCALE = float(HEAD) ** -0.5

    ctx = ExitStack()
    attn_ctx = ExitStack()
    ffn_ctx = ExitStack()
    with ctx:
        def sb(where, name, shape, dt=f32):
            return where.enter_context(nc.sbuf_tensor(name, shape, dt))

        def sem(name):
            return ctx.enter_context(nc.semaphore(name))

        def bank(name, banks=1):
            return ctx.enter_context(nc.psum_tensor(name, [P, CHUNK * banks], f32))

        rows = sb(ctx, "rows", [P, ALL_BLOCKS, DIM])
        id_sb = sb(ctx, "id_sb", [P, P])
        ffn_raw = sb(ctx, "ffn_raw", [P, 3, CHUNK])
        lora_sb = sb(ctx, "lora_sb", [RANK, 3, P])
        lora_full = sb(ctx, "lora_full", [RANK, 3, DIM])
        stats = sb(ctx, "stats", [P, BPC, 6])
        moments = sb(ctx, "moments", [P, BPC, 2])
        var_eps = sb(ctx, "var_eps", [P, BPC])
        minus_half = sb(ctx, "minus_half", [P, BPC])
        rstd0 = sb(ctx, "rstd0", [P, BPC])
        newton = sb(ctx, "newton", [P, 3, BPC])
        rstd = sb(ctx, "rstd", [P, BPC])

        x_raw = sb(attn_ctx, "x_raw", [P, KD, CHUNK])
        x_hi = sb(attn_ctx, "x_hi", [P, 2, KD, CHUNK], f32r)
        x_lo = sb(attn_ctx, "x_lo", [P, 2, KD, CHUNK], f32r)
        w_raw = sb(attn_ctx, "w_raw", [P, RING, CHUNK])
        w_hi = sb(attn_ctx, "w_hi", [P, PIECES, CHUNK], f32r)
        w_lo = sb(attn_ctx, "w_lo", [P, PIECES, CHUNK], f32r)
        cos_sin = sb(attn_ctx, "cos_sin", [P, 2, SEQ])
        later_sb = sb(attn_ctx, "later_sb", [P, P], i32)
        none_before = sb(attn_ctx, "none_before", [P, P])
        swapped = sb(attn_ctx, "swapped", [P, 2, CHUNK])
        by_cos = sb(attn_ctx, "by_cos", [P, CHUNK])
        q_rot = sb(attn_ctx, "q_rot", [P, 2, GROUP, CHUNK])
        k_rot = sb(attn_ctx, "k_rot", [P, SEQ])
        v_cols = sb(attn_ctx, "v_cols", [P, CHUNK])
        v_hi = sb(attn_ctx, "v_hi", [P, BLOCKS, HEAD], f32r)
        v_lo = sb(attn_ctx, "v_lo", [P, BLOCKS, HEAD], f32r)
        neg_max = sb(attn_ctx, "neg_max", [P, GROUP])
        exp_bias = sb(attn_ctx, "exp_bias", [P, GROUP])
        sums = sb(attn_ctx, "sums", [P, GROUP])
        inv_sums = sb(attn_ctx, "inv_sums", [P, GROUP])
        probs = sb(attn_ctx, "probs", [P, GROUP, P])
        pt_hi = sb(attn_ctx, "pt_hi", [P, GROUP, P])
        pt_lo = sb(attn_ctx, "pt_lo", [P, GROUP, P])
        masked = sb(attn_ctx, "masked", [P, 4, CHUNK], f32r)
        o_hi = sb(attn_ctx, "o_hi", [P, CHUNK], f32r)
        o_lo = sb(attn_ctx, "o_lo", [P, CHUNK], f32r)
        attn_ctx.close()

        y_hi = sb(ffn_ctx, "y_hi", [P, KD, BATCH * SEQ], f32r)
        y_lo = sb(ffn_ctx, "y_lo", [P, KD, BATCH * SEQ], f32r)
        merged = sb(ffn_ctx, "merged", [P, 3, CHUNK])
        fw_hi = sb(ffn_ctx, "fw_hi", [P, 3, CHUNK], f32r)
        fw_lo = sb(ffn_ctx, "fw_lo", [P, 3, CHUNK], f32r)
        silu = sb(ffn_ctx, "silu", [P, CHUNK])
        gate = sb(ffn_ctx, "gate", [P, CHUNK])
        g_hi = sb(ffn_ctx, "g_hi", [P, 2, CHUNK], f32r)
        g_lo = sb(ffn_ctx, "g_lo", [P, 2, CHUNK], f32r)
        ffn_ctx.close()

        ps_proj = [bank("ps_proj0"), bank("ps_proj1")]
        ps_scores = bank("ps_scores", 2)
        ps_pt, ps_o, ps_out, ps_v = bank("ps_pt"), bank("ps_o"), bank("ps_out"), bank("ps_v")
        ps_h1, ps_h3 = ps_proj
        ps_lora = ps_pt
        ps_yt = [ps_pt, ps_v]
        down_banks = [ps_scores[:, 0:CHUNK], ps_scores[:, CHUNK:2 * CHUNK], ps_o[:, :], ps_out[:, :]]
        scores = ps_scores[:, :].rearrange("p (h c) -> p h c", h=GROUP)

        x_loaded, rows_loaded, rope_loaded = [sem(f"x_loaded{k}") for k in range(KD)], sem("rows_loaded"), sem("rope_loaded")
        w_loaded = [sem(f"w_loaded{r}") for r in range(RING)]
        consts_loaded, const_set = sem("consts_loaded"), sem("const_set")
        x_hi_done, x_split = sem("x_hi_done"), sem("x_split")
        w_hi_done, w_split = sem("w_hi_done"), sem("w_split")
        proj_done, v_turned, scores_done, pt_done = sem("proj_done"), sem("v_turned"), sem("scores_done"), sem("pt_done")
        pv_done, out_done = sem("pv_done"), sem("out_done")
        halves_swapped, by_cos_done, by_sin_done, rotated = sem("halves_swapped"), sem("by_cos_done"), sem("by_sin_done"), sem("rotated")
        v_copied, v_hi_done, v_split = sem("v_copied"), sem("v_hi_done"), sem("v_split")
        row_merged, max_done, bias_done, exp_done = sem("row_merged"), sem("max_done"), sem("bias_done"), sem("exp_done")
        inv_done, probs_done = sem("inv_done"), sem("probs_done")
        pt_hi_done, pt_split, masks_done = sem("pt_hi_done"), sem("pt_split"), sem("masks_done")
        o_hi_done, o_split, rows_added = sem("o_hi_done"), sem("o_split"), sem("rows_added")
        stats_done, moments_done, var_done, pow_done = sem("stats_done"), sem("moments_done"), sem("var_done"), sem("pow_done")
        newton_done, normed = sem("newton_done"), sem("normed")
        y_turned, y_hi_done, y_split = sem("y_turned"), sem("y_hi_done"), sem("y_split")
        ffn_loaded = [sem(f"ffn_loaded{p}") for p in range(3)]
        lora_loaded, lora_done, merge_done = sem("lora_loaded"), sem("lora_done"), sem("merge_done")
        fw_hi_done, fw_split = sem("fw_hi_done"), sem("fw_split")
        h1_done, h3_done, silu_done, gate_done, g_hi_done, g_split = (
            sem("h1_done"), sem("h3_done"), sem("silu_done"), sem("gate_done"), sem("g_hi_done"), sem("g_split"))
        down_done, ffn_added, stored = sem("down_done"), sem("ffn_added"), sem("stored")

        def iterations(eng, body):
            body(0, 0, True, False)
            with eng.Fori(1, KV_HEADS - 1) as i:
                body(i, 0, False, False)
            body(KV_HEADS - 1, 0, False, False)
            body(KV_HEADS, 1, False, False)
            with eng.Fori(KV_HEADS + 1, ITERS - 1) as i:
                body(i, 1, False, False)
            body(ITERS - 1, 1, False, True)

        def hidden_tiles(eng, body):
            body(0, True, False)
            with eng.Fori(1, HT - 1) as ht:
                body(ht, False, False)
            body(HT - 1, False, True)

        def next_chunk(I, j):
            return 2 * I + 1 + j // BPC

        def piece_number(I, p):
            return PROJ + PIECES * I + p

        block = ctx.enter_context(nc.Block())

        @block.sync
        def _(sp):
            def load_x(c):
                for k in range(KD):
                    if c:
                        sp.wait_ge(x_split, KD * (c - 1) + k + 1)
                    sp.dma_start(x_raw[:, k, :], x_cols[c, :, k, :]).then_inc(x_loaded[k], 16)

            def load_w(I, p, row):
                number = piece_number(I, p)
                sp.wait_ge(w_split, number - RING + 1)
                sp.dma_start(w_raw[:, (PROJ + p) % RING, :], attn_w[row]).then_inc(w_loaded[(PROJ + p) % RING], 16)

            first_row = PIECES * (KV_HEADS - 1) + WO_PIECES
            sp.dma_start(w_raw[:, 0, :], attn_w[first_row]).then_inc(w_loaded[0], 16)
            load_x(0)
            for p in range(1, RING):
                sp.dma_start(w_raw[:, p, :], attn_w[first_row + p]).then_inc(w_loaded[p], 16)
            sp.dma_start(cos_sin[:, :, :], rope).then_inc(rope_loaded, 16)
            sp.dma_start(id_sb[:, :], ident).then_inc(consts_loaded, 16)
            sp.dma_start(later_sb[:, :], later).then_inc(consts_loaded, 16)
            sp.wait_ge(w_split, 1)
            sp.dma_start(w_raw[:, 0, :], attn_w[first_row + RING]).then_inc(w_loaded[0], 16)
            load_x(1)
            sp.dma_start(rows[:, :, :], x_rows).then_inc(rows_loaded, 16)
            sp.dma_start(lora_full[:, :, :], lora_all).then_inc(lora_loaded, 16)
            sp.dma_start(lora_sb[:, :, :], lora_tile[0]).then_inc(lora_loaded, 16)
            for p in range(3):
                sp.dma_start(ffn_raw[:, p, :], ffn_w[p]).then_inc(ffn_loaded[p], 16)
            load_x(2)

            def body(I, batch, first, last):
                for p in range(WO_PIECES if last else PIECES):
                    load_w(I, p, PIECES * (I - KV_HEADS * batch) + p)
                if not isinstance(I, int):
                    return
                if I == KV_HEADS - 1:
                    load_x(3)
            iterations(sp, body)

            def ffn_body(ht, first, last):
                if last:
                    return
                for p in range(3):
                    sp.wait_ge(merge_done, 3 * ht + p + 1)
                    sp.dma_start(ffn_raw[:, p, :], ffn_w[3 * (ht + 1) + p]).then_inc(ffn_loaded[p], 16)
                sp.dma_start(lora_sb[:, :, :], lora_tile[ht + 1]).then_inc(lora_loaded, 16)
            hidden_tiles(sp, ffn_body)
            for c in range(CHUNKS):
                sp.wait_ge(normed, BPC * (CHUNKS + c + 1))
                sp.dma_start(out[:, BPC * c:BPC * (c + 1), :], rows[:, BPC * c:BPC * (c + 1), :]).then_inc(stored, 16)
            sp.wait_ge(stored, 16 * CHUNKS)

        @block.tensor
        def _(pe):
            def three(out_, a, b, start, stop):
                pe.matmul(out_, a[0], b[0], start=start, stop=False)
                pe.matmul(out_, a[0], b[1], start=False, stop=False)
                return pe.matmul(out_, a[1], b[0], start=False, stop=stop)

            def project(I, C, parity, p):
                pe.wait_ge(w_split, PIECES * I + p + 1)
                if p == 0:
                    bank_free, count = by_cos_done, ROPES * C
                elif p == 1:
                    bank_free, count = v_copied, C
                else:
                    bank_free, count = by_cos_done, ROPES * C + p - 1
                if not (isinstance(C, int) and C == 0 and p < 2):
                    pe.wait_ge(bank_free, count)
                w = WO_PIECES + p
                for k in range(KD):
                    if isinstance(C, int) and C == 0 and p == 0:
                        pe.wait_ge(x_split, k + 1)
                    cols = slice(k * P, (k + 1) * P)
                    mm = three(ps_proj[p % 2][:, :], (w_hi[:, w, cols], w_lo[:, w, cols]),
                               (x_hi[:, parity, k, :], x_lo[:, parity, k, :]), k == 0, k == KD - 1)
                mm.then_inc(proj_done, 1)

            def turn_v(C):
                pe.wait_ge(v_copied, C + 1)
                if not (isinstance(C, int) and C == 0):
                    pe.wait_ge(v_split, C)
                for t in range(BPC):
                    mm = pe.transpose(ps_v[:, t * P:(t + 1) * P], v_cols[:, t * P:(t + 1) * P], id_sb[:, :])
                mm.then_inc(v_turned, 1)

            def score(n, j):
                c = (j // BPC) % 2
                pe.wait_ge(rotated, ROPES * (n // BPC + 1) if isinstance(n, int) else ROPES * chunk_of[0] + ROPES)
                if not (isinstance(n, int) and n == 0):
                    pe.wait_ge(exp_done, n)
                t = j % BPC
                for h in range(GROUP):
                    q = q_rot[:, c, h, t * P:(t + 1) * P]
                    if j == 0:
                        mm = pe.matmul(scores[:, h, P:2 * P], q, k_rot[:, 0:P], start=True, stop=True)
                    else:
                        mm = pe.matmul(scores[:, h, :], q, k_rot[:, (j - 1) * P:(j + 1) * P], start=True, stop=True)
                mm.then_inc(scores_done, 1)

            def turn_probs(n):
                pe.wait_ge(probs_done, n + 1)
                if not (isinstance(n, int) and n == 0):
                    pe.wait_ge(pt_split, n)
                for h in range(GROUP):
                    mm = pe.transpose(ps_pt[:, h * P:(h + 1) * P], probs[:, h, :], id_sb[:, :])
                mm.then_inc(pt_done, 1)

            def values(n, j):
                pe.wait_ge(masks_done, 4 * (n + 1))
                if j % BPC == 0:
                    pe.wait_ge(v_split, chunk_of[0] + 1)
                if not (isinstance(n, int) and n == 0):
                    pe.wait_ge(o_split, n)
                if j:
                    three(ps_o[:, :], (v_hi[:, j - 1, :], v_lo[:, j - 1, :]), (masked[:, 1, :], masked[:, 3, :]), True, False)
                three(ps_o[:, :], (v_hi[:, j, :], v_lo[:, j, :]), (masked[:, 0, :], masked[:, 2, :]), j == 0, True)\
                    .then_inc(pv_done, 1)

            def output(n, I):
                pe.wait_ge(w_split, piece_number(I, WO_PIECES))
                pe.wait_ge(o_split, n + 1)
                if not (isinstance(n, int) and n == 0):
                    pe.wait_ge(rows_added, n)
                for h in range(GROUP):
                    cols = slice(h * P, (h + 1) * P)
                    mm = three(ps_out[:, :], (o_hi[:, cols], o_lo[:, cols]), (w_hi[:, h, :], w_lo[:, h, :]),
                               h == 0, h == GROUP - 1)
                mm.then_inc(out_done, 1)

            chunk_of = [0]

            for p in range(PROJ):
                project(0, 0, 0, p)
            pe.wait_ge(consts_loaded, 32)
            turn_v(0)

            def body(I, batch, first, last):
                for j in range(BLOCKS):
                    n = BLOCKS * I + j
                    C = next_chunk(I, j)
                    early, late = EARLY[j % BPC], LATE[j % BPC]
                    weights_of = I + j // BPC
                    projects = not (last and j >= BPC)
                    if projects:
                        if batch == 0 and isinstance(I, int) and j % BPC == 0:
                            if first and j == 0:
                                pe.wait_ge(x_split, 2 * KD)
                            if I == KV_HEADS - 1 and j == BPC:
                                pe.wait_ge(x_split, 3 * KD)
                        if batch == 1 and j == 0:
                            pe.wait_ge(x_split, 4 * KD)
                        project(weights_of, C, (j // BPC + 1) % 2, early)
                    if not (first and j == 0):
                        turn_probs(n - 1)
                    chunk_of[0] = 2 * I + j // BPC
                    score(n, j)
                    if not (first and j < 2):
                        output(n - 2, I if j >= 2 else I - 1)
                    if not (first and j == 0):
                        chunk_of[0] = 2 * I + (j - 1) // BPC
                        values(n - 1, (j - 1) % BLOCKS)
                    if projects and late is not None:
                        project(weights_of, C, (j // BPC + 1) % 2, late)
                    if projects and early == V_PROJ:
                        turn_v(C)
            iterations(pe, body)
            n = BLOCKS * ITERS
            turn_probs(n - 1)
            output(n - 2, ITERS - 1)
            values(n - 1, BLOCKS - 1)
            output(n - 1, ITERS - 1)

            def adapter(ht, p):
                number = 3 * ht + p
                if p == 0:
                    pe.wait_ge(lora_loaded, 16 * (ht + 2))
                if not (isinstance(number, int) and number == 0):
                    pe.wait_ge(merge_done, number)
                if p < 2:
                    for k in range(KD):
                        mm = pe.matmul(ps_lora[:, k * P:(k + 1) * P], lora_full[:, p, k * P:(k + 1) * P],
                                       lora_sb[:, p, :], start=True, stop=True)
                else:
                    mm = pe.matmul(ps_lora[:, :], lora_sb[:, 2, :], lora_full[:, 2, :], start=True, stop=True)
                mm.then_inc(lora_done, 1)

            def turn_y(m):
                for b in range(BPC * m, BPC * (m + 1)):
                    pe.wait_ge(normed, b + 1)
                    if b >= 2:
                        pe.wait_ge(y_split, b - 1)
                    if b % 2 == 0:
                        pe.wait_ge(merge_done, 4 if m == CHUNKS - 1 else 3)
                    for k in range(KD):
                        mm = pe.transpose(ps_yt[b % 2][:, k * P:(k + 1) * P], rows[:, b, k * P:(k + 1) * P], id_sb[:, :])
                    mm.then_inc(y_turned, 1)

            def up(ht, m, p, ps, done):
                M = CHUNKS * ht + m
                pe.wait_ge(fw_split, 3 * ht + p + 1)
                if not (isinstance(M, int) and M == 0):
                    pe.wait_ge(gate_done if p else silu_done, M)
                for k in range(KD):
                    cols = slice(k * P, (k + 1) * P)
                    mm = three(ps[:, :], (fw_hi[:, p, cols], fw_lo[:, p, cols]),
                               (y_hi[:, k, m * CHUNK:(m + 1) * CHUNK], y_lo[:, k, m * CHUNK:(m + 1) * CHUNK]),
                               k == 0, k == KD - 1)
                mm.then_inc(done, 1)

            def down(ht, m):
                M = CHUNKS * ht + m
                pe.wait_ge(fw_split, 3 * ht + 3)
                pe.wait_ge(g_split, M + 1)
                for t in range(BPC):
                    if not (isinstance(M, int) and M == 0):
                        pe.wait_ge(ffn_added, BPC * (M - 1) + t + 1)
                    cols = slice(t * P, (t + 1) * P)
                    three(down_banks[t], (g_hi[:, m % 2, cols], g_lo[:, m % 2, cols]),
                          (fw_hi[:, 2, :], fw_lo[:, 2, :]), True, True).then_inc(down_done, 1)

            for p in range(3):
                adapter(0, p)
            turn_y(0)

            def ffn_body(ht, first, last):
                for m in range(CHUNKS):
                    if first:
                        pe.wait_ge(y_split, BPC * (m + 1))
                    up(ht, m, 0, ps_h1, h1_done)
                    up(ht, m, 1, ps_h3, h3_done)
                    if first and m + 1 < CHUNKS:
                        turn_y(m + 1)
                    if not (first and m == 0):
                        if m:
                            down(ht, m - 1)
                        else:
                            down(ht - 1, CHUNKS - 1)
                    if not last and m:
                        if first:
                            pe.wait_ge(y_split, BPC * min(m + 2, CHUNKS))
                        adapter(ht + 1, m - 1)
            hidden_tiles(pe, ffn_body)
            down(HT - 1, CHUNKS - 1)

        @block.scalar
        def _(act):
            def split_x(c, k):
                act.wait_ge(x_loaded[k], 16 * (c + 1))
                if c >= 2:
                    act.wait_ge(proj_done, PROJ * (2 * KV_HEADS - 3 + c))
                act.activation(x_hi[:, c % 2, k, :], x_raw[:, k, :], ACT.Copy).then_inc(x_hi_done, 1)

            def split_w(I, p):
                number = piece_number(I, p)
                act.wait_ge(w_loaded[(PROJ + p) % RING], 16 * (2 * I + (PROJ + p) // RING + 1))
                if p < WO_PIECES:
                    if not (isinstance(I, int) and I == 0):
                        act.wait_ge(out_done, BLOCKS * I)
                else:
                    act.wait_ge(proj_done, PROJ * (2 * I + 1) + p - WO_PIECES + 1)
                act.activation(w_hi[:, p, :], w_raw[:, (PROJ + p) % RING, :], ACT.Copy).then_inc(w_hi_done, 1)

            def swap_halves(C, p):
                act.wait_ge(proj_done, PROJ * C + p + 1)
                if p >= 2:
                    act.wait_ge(rotated, ROPES * C + p - 1)
                elif not (isinstance(C, int) and C == 0):
                    act.wait_ge(rotated, ROPES * C if p == 0 else ROPES * C - 1)
                half = HEAD // 2
                act.activation(swapped[0:half, p % 2, :], ps_proj[p % 2][half:HEAD, :], ACT.Copy)
                act.activation(swapped[half:HEAD, p % 2, :], ps_proj[p % 2][0:half, :], ACT.Copy).then_inc(halves_swapped, 1)

            def copy_v(C):
                act.wait_ge(proj_done, PROJ * (C + 1))
                if not (isinstance(C, int) and C == 0):
                    act.wait_ge(v_turned, C)
                act.activation(v_cols[:, :], ps_proj[V_PROJ % 2][:, :], ACT.Copy).then_inc(v_copied, 1)

            def split_v(C, parity):
                act.wait_ge(v_turned, C + 1)
                act.activation(v_hi[:, parity * BPC:(parity + 1) * BPC, :],
                               ps_v[:, :].rearrange("p (t d) -> p t d", t=BPC), ACT.Copy).then_inc(v_hi_done, 1)

            def split_pt(n):
                act.wait_ge(pt_done, n + 1)
                if not (isinstance(n, int) and n == 0):
                    act.wait_ge(masks_done, 4 * n)
                act.activation(pt_hi[:, :, :].bitcast(f32r), ps_pt[:, :].rearrange("p (h q) -> p h q", h=GROUP),
                               ACT.Copy).then_inc(pt_hi_done, 1)

            def exponentials(n):
                act.wait_ge(bias_done, n + 1)
                if not (isinstance(n, int) and n == 0):
                    act.wait_ge(pt_done, n)
                for h in range(GROUP):
                    e = act.activation(probs[:, h, :], scores[:, h, P:2 * P], ACT.Exp, bias=exp_bias[:, h:h + 1],
                                       scale=SCALE, accum_out=sums[:, h:h + 1])
                e.then_inc(exp_done, 1)

            def split_o(n):
                act.wait_ge(pv_done, n + 1)
                if not (isinstance(n, int) and n == 0):
                    act.wait_ge(out_done, n)
                act.activation(o_hi[:, :], ps_o[:, :], ACT.Copy).then_inc(o_hi_done, 1)

            def first_w(p):
                act.wait_ge(w_loaded[p % RING], 16 * (p // RING + 1))
                act.activation(w_hi[:, WO_PIECES + p, :], w_raw[:, p % RING, :], ACT.Copy).then_inc(w_hi_done, 1)

            first_w(0)
            for k in range(KD):
                split_x(0, k)
            for p in range(1, PROJ):
                first_w(p)
            for p in range(ROPES):
                swap_halves(0, p)
            copy_v(0)
            split_v(0, 0)
            for k in range(KD):
                split_x(1, k)

            def body(I, batch, first, last):
                for j in range(BLOCKS):
                    n = BLOCKS * I + j
                    C = next_chunk(I, j)
                    early, late = EARLY[j % BPC], LATE[j % BPC]
                    projects = not (last and j >= BPC)
                    if not (first and j == 0):
                        split_pt(n - 1)
                    if projects:
                        if early == V_PROJ:
                            copy_v(C)
                        else:
                            swap_halves(C, early)
                    exponentials(n)
                    if not (first and j == 0):
                        split_o(n - 1)
                    for p in SPLITS.get(j, []):
                        if not (last and p >= WO_PIECES):
                            split_w(I, p)
                    if projects and late is not None:
                        swap_halves(C, late)
                    if projects and early == V_PROJ:
                        split_v(C, (j // BPC + 1) % 2)
                    if isinstance(I, int) and I == KV_HEADS - 1:
                        split_x(2 + j // BPC, j % BPC)
            iterations(act, body)
            n = BLOCKS * ITERS
            split_pt(n - 1)
            split_o(n - 1)

            def split_fw(ht, p):
                act.wait_ge(merge_done, 3 * ht + p + 1)
                if not (isinstance(ht, int) and ht == 0):
                    act.wait_ge([h1_done, h3_done, down_done][p], (BPC if p == 2 else 1) * CHUNKS * ht)
                act.activation(fw_hi[:, p, :], merged[:, p, :], ACT.Copy).then_inc(fw_hi_done, 1)

            def split_y(m):
                for b in range(BPC * m, BPC * (m + 1)):
                    act.wait_ge(y_turned, b + 1)
                    act.activation(y_hi[:, :, b * P:(b + 1) * P],
                                   ps_yt[b % 2][:, :].rearrange("p (k t) -> p k t", k=KD), ACT.Copy).then_inc(y_hi_done, 1)

            for p in range(3):
                split_fw(0, p)
            split_y(0)

            def ffn_body(ht, first, last):
                for m in range(CHUNKS):
                    M = CHUNKS * ht + m
                    act.wait_ge(h1_done, M + 1)
                    if not (first and m == 0):
                        act.wait_ge(gate_done, M)
                    act.activation(silu[:, :], ps_h1[:, :], ACT.Silu).then_inc(silu_done, 1)
                    if not last and m == CHUNKS - 1:
                        split_fw(ht + 1, 0)
                    act.wait_ge(gate_done, M + 1)
                    if not (first and m < 2):
                        act.wait_ge(down_done, BPC * (M - 1))
                    act.activation(g_hi[:, m % 2, :], gate[:, :], ACT.Copy).then_inc(g_hi_done, 1)
                    if first and m + 1 < CHUNKS:
                        split_y(m + 1)
                    if not last and m == CHUNKS - 1:
                        split_fw(ht + 1, 1)
                    if not first and m == 0:
                        split_fw(ht, 2)
            hidden_tiles(act, ffn_body)

        @block.gpsimd
        def _(pool):
            pool.memset(minus_half[:, :], -0.5).then_inc(const_set, 1)
            pool.wait_ge(rope_loaded, 16)

            def by_sin(C, p, parity):
                pool.wait_ge(halves_swapped, ROPES * C + p + 1)
                pool.tensor_tensor(swapped[:, p % 2, :], swapped[:, p % 2, :],
                                   cos_sin[:, 1, parity * CHUNK:(parity + 1) * CHUNK], ALU.mult).then_inc(by_sin_done, 1)

            def mask(n):
                for part, src, ready in ((0, pt_hi, pt_hi_done), (2, pt_lo, pt_split)):
                    counts = [n, n + 1] if isinstance(n, int) else [pool.to_reg(n), pool.to_reg(n + 1)]
                    pool.wait_ge(const_set, 1)
                    pool.wait_ge(ready, counts[1])
                    if part == 0 and not (isinstance(n, int) and n == 0):
                        pool.wait_ge(pv_done, counts[0])
                    for before in range(2):
                        sign = -1 if before else 1
                        pool.affine_select(
                            out=masked[:, part + before, :].rearrange("p (h q) -> p h q", h=GROUP),
                            in_=src[:, :, :], compare_op=ALU.is_ge, fill=0.0, base=-before,
                            pattern=[[0, GROUP], [sign, P]], channel_multiplier=-sign).then_inc(masks_done, 1)

            for p in range(ROPES):
                by_sin(0, p, 0)

            def body(I, batch, first, last):
                for j in range(BLOCKS):
                    n = BLOCKS * I + j
                    C = next_chunk(I, j)
                    early, late = EARLY[j % BPC], LATE[j % BPC]
                    projects = not (last and j >= BPC)
                    if not (first and j == 0):
                        mask(n - 1)
                    if projects and early != V_PROJ:
                        by_sin(C, early, (j // BPC + 1) % 2)
                    if projects and late is not None:
                        by_sin(C, late, (j // BPC + 1) % 2)
            iterations(pool, body)
            mask(BLOCKS * ITERS - 1)
            for call in range(2 * CHUNKS):
                pool.wait_ge(var_done, call + 1)
                if call == 0:
                    pool.wait_ge(const_set, 1)
                pool.tensor_tensor(rstd0[:, :], var_eps[:, :], minus_half[:, :], ALU.pow).then_inc(pow_done, 1)

        @block.vector
        def _(dve):
            def low(out_, full, hi, done):
                dve.tensor_tensor(out_, full, hi, ALU.subtract).then_inc(done, 1)

            def split_x(c, k):
                dve.wait_ge(x_hi_done, KD * c + k + 1)
                low(x_lo[:, c % 2, k, :], x_raw[:, k, :], x_hi[:, c % 2, k, :].bitcast(f32), x_split)

            def split_w(I, p):
                dve.wait_ge(w_hi_done, piece_number(I, p) + 1)
                low(w_lo[:, p, :], w_raw[:, (PROJ + p) % RING, :], w_hi[:, p, :].bitcast(f32), w_split)

            def by_cos_(C, p, parity):
                dve.wait_ge(halves_swapped, ROPES * C + p + 1)
                if not (isinstance(C, int) and C == 0 and p == 0):
                    dve.wait_ge(rotated, ROPES * C + p)
                dve.tensor_tensor(by_cos[:, :], ps_proj[p % 2][:, :],
                                  cos_sin[:, 0, parity * CHUNK:(parity + 1) * CHUNK], ALU.mult).then_inc(by_cos_done, 1)

            def rotate(C, p, parity):
                dve.wait_ge(by_cos_done, ROPES * C + p + 1)
                dve.wait_ge(by_sin_done, ROPES * C + p + 1)
                if not (isinstance(C, int) and C < 2):
                    dve.wait_ge(scores_done, BPC * (C - 1) + (p == K_PROJ))
                place = k_rot[:, parity * CHUNK:(parity + 1) * CHUNK] if p == K_PROJ else q_rot[:, parity, p, :]
                dve.tensor_tensor(place, by_cos[:, :], swapped[:, p % 2, :], ALU.add).then_inc(rotated, 1)

            def split_v(C, parity):
                dve.wait_ge(v_hi_done, C + 1)
                blocks = slice(parity * BPC, (parity + 1) * BPC)
                low(v_lo[:, blocks, :], ps_v[:, :].rearrange("p (t d) -> p t d", t=BPC), v_hi[:, blocks, :].bitcast(f32), v_split)

            def split_pt(n):
                dve.wait_ge(pt_hi_done, n + 1)
                low(pt_lo[:, :, :], ps_pt[:, :].rearrange("p (h q) -> p h q", h=GROUP), pt_hi[:, :, :], pt_split)

            def row_max(n, j):
                count = n + 1 if isinstance(n, int) else dve.to_reg(n + 1)
                dve.wait_ge(consts_loaded, 32)
                dve.wait_ge(scores_done, count)
                slot_after = later_sb[:, :].unsqueeze(1).broadcast_to([P, GROUP, P])
                before = scores[:, :, 0:P] if j else none_before[:, :].unsqueeze(1).broadcast_to([P, GROUP, P])
                dve.copy_predicated(scores[:, :, P:2 * P], slot_after, before).then_inc(row_merged, 1)
                dve.wait_ge(row_merged, n + 1)
                dve.tensor_reduce(neg_max[:, :], scores[:, :, P:2 * P], AX.X, ALU.max, negate=True).then_inc(max_done, 1)
                dve.wait_ge(max_done, n + 1)
                dve.tensor_scalar(exp_bias[:, :], neg_max[:, :], SCALE, None, ALU.mult).then_inc(bias_done, 1)

            def normalise(n):
                dve.wait_ge(exp_done, n + 1)
                dve.reciprocal(inv_sums[:, :], sums[:, :]).then_inc(inv_done, 1)
                dve.wait_ge(inv_done, n + 1)
                dve.tensor_tensor(probs[:, :, :], probs[:, :, :], inv_sums[:, :].unsqueeze(2).broadcast_to([P, GROUP, P]),
                                  ALU.mult).then_inc(probs_done, 1)

            def add_rows(n, b):
                dve.wait_ge(out_done, n + 1)
                dve.tensor_tensor(rows[:, b, :], ps_out[:, :], rows[:, b, :], ALU.add).then_inc(rows_added, 1)

            def split_o(n):
                dve.wait_ge(o_hi_done, n + 1)
                low(o_lo[:, :], ps_o[:, :], o_hi[:, :].bitcast(f32), o_split)

            def first_w(p):
                dve.wait_ge(w_hi_done, p + 1)
                low(w_lo[:, WO_PIECES + p, :], w_raw[:, p % RING, :], w_hi[:, WO_PIECES + p, :].bitcast(f32), w_split)

            dve.memset(none_before[:, :], NEG).then_inc(const_set, 1)
            first_w(0)
            for k in range(KD):
                split_x(0, k)
            for p in range(1, PROJ):
                first_w(p)
            dve.wait_ge(rope_loaded, 16)
            dve.wait_ge(const_set, 2)
            for p in range(ROPES):
                by_cos_(0, p, 0)
                rotate(0, p, 0)
            split_v(0, 0)
            for k in range(KD):
                split_x(1, k)
            dve.wait_ge(rows_loaded, 16)

            def body(I, batch, first, last):
                for j in range(BLOCKS):
                    n = BLOCKS * I + j
                    C = next_chunk(I, j)
                    parity = (j // BPC + 1) % 2
                    early, late = EARLY[j % BPC], LATE[j % BPC]
                    projects = not (last and j >= BPC)
                    if not (first and j == 0):
                        split_pt(n - 1)
                    rotates = projects and early != V_PROJ
                    if rotates:
                        by_cos_(C, early, parity)
                    row_max(n, j)
                    normalise(n)
                    if not (first and j < 2):
                        before = j < 2 and isinstance(I, int) and I == KV_HEADS
                        add_rows(n - 2, BLOCKS * (batch - before) + (j - 2) % BLOCKS)
                    if rotates:
                        rotate(C, early, parity)
                    if not (first and j == 0):
                        split_o(n - 1)
                    for p in SPLITS.get(j, []):
                        if not (last and p >= WO_PIECES):
                            split_w(I, p)
                    if projects and late is not None:
                        by_cos_(C, late, parity)
                        rotate(C, late, parity)
                    if projects and early == V_PROJ:
                        split_v(C, parity)
                    if isinstance(I, int) and I == KV_HEADS - 1:
                        split_x(2 + j // BPC, j % BPC)
            iterations(dve, body)
            n = BLOCKS * ITERS
            split_pt(n - 1)
            add_rows(n - 2, ALL_BLOCKS - 2)
            split_o(n - 1)
            add_rows(n - 1, ALL_BLOCKS - 1)

            def layer_norm(call, m):
                if call < CHUNKS:
                    dve.wait_ge(rows_added, BLOCKS * ITERS)
                else:
                    dve.wait_ge(ffn_added, BPC * (CHUNKS * (HT - 1) + m + 1))
                blocks = range(BPC * m, BPC * (m + 1))
                for t, b in enumerate(blocks):
                    dve.bn_stats(stats[:, t, :], rows[:, b, :]).then_inc(stats_done, 1)
                for t in range(BPC):
                    dve.wait_ge(stats_done, BPC * call + t + 1)
                    dve.bn_aggr(moments[:, t, :], stats[:, t, :]).then_inc(moments_done, 1)
                dve.wait_ge(moments_done, BPC * (call + 1))
                dve.tensor_scalar(var_eps[:, :], moments[:, :, 1], EPS, None, ALU.add).then_inc(var_done, 1)
                dve.wait_ge(pow_done, call + 1)
                dve.tensor_tensor(newton[:, 0, :], rstd0[:, :], rstd0[:, :], ALU.mult).then_inc(newton_done, 1)
                dve.wait_ge(newton_done, 4 * call + 1)
                dve.tensor_tensor(newton[:, 1, :], newton[:, 0, :], var_eps[:, :], ALU.mult).then_inc(newton_done, 1)
                dve.wait_ge(newton_done, 4 * call + 2)
                dve.tensor_scalar(newton[:, 2, :], newton[:, 1, :], -0.5, 1.5, ALU.mult, ALU.add).then_inc(newton_done, 1)
                dve.wait_ge(newton_done, 4 * call + 3)
                dve.tensor_tensor(rstd[:, :], newton[:, 2, :], rstd0[:, :], ALU.mult).then_inc(newton_done, 1)
                dve.wait_ge(newton_done, 4 * call + 4)
                for t, b in enumerate(blocks):
                    dve.tensor_scalar(rows[:, b, :], rows[:, b, :], moments[:, t, 0:1], rstd[:, t:t + 1],
                                      ALU.subtract, ALU.mult).then_inc(normed, 1)

            def merge(ht, p):
                dve.wait_ge(lora_done, 3 * ht + p + 1)
                dve.wait_ge(ffn_loaded[p], 16 * (ht + 1))
                if not (isinstance(ht, int) and ht == 0):
                    dve.wait_ge(fw_split, 3 * (ht - 1) + p + 1)
                dve.scalar_tensor_tensor(out=merged[:, p, :], in0=ps_lora[:, :], scalar=LORA_SCALE, in1=ffn_raw[:, p, :],
                                         op0=ALU.mult, op1=ALU.add).then_inc(merge_done, 1)

            def split_fw(ht, p):
                dve.wait_ge(fw_hi_done, 3 * ht + p + 1)
                low(fw_lo[:, p, :], merged[:, p, :], fw_hi[:, p, :].bitcast(f32), fw_split)

            def split_y(m):
                for b in range(BPC * m, BPC * (m + 1)):
                    dve.wait_ge(y_hi_done, b + 1)
                    cols = slice(b * P, (b + 1) * P)
                    low(y_lo[:, :, cols], ps_yt[b % 2][:, :].rearrange("p (k t) -> p k t", k=KD),
                        y_hi[:, :, cols].bitcast(f32), y_split)

            def add_ffn(ht, m):
                M = CHUNKS * ht + m
                for t in range(BPC):
                    dve.wait_ge(down_done, BPC * M + t + 1)
                    b = BPC * m + t
                    dve.tensor_tensor(rows[:, b, :], down_banks[t], rows[:, b, :], ALU.add).then_inc(ffn_added, 1)

            layer_norm(0, 0)
            for p in range(3):
                merge(0, p)
            for p in range(3):
                split_fw(0, p)
            split_y(0)

            def ffn_body(ht, first, last):
                for m in range(CHUNKS):
                    M = CHUNKS * ht + m
                    if first and m + 1 < CHUNKS:
                        layer_norm(m + 1, m + 1)
                    if not last and m == CHUNKS - 1:
                        split_fw(ht + 1, 0)
                    dve.wait_ge(silu_done, M + 1)
                    dve.wait_ge(h3_done, M + 1)
                    if not (first and m == 0):
                        dve.wait_ge(g_split, M)
                    dve.tensor_tensor(gate[:, :], ps_h3[:, :], silu[:, :], ALU.mult).then_inc(gate_done, 1)
                    if first and m + 1 < CHUNKS:
                        split_y(m + 1)
                    if not (first and m == 0):
                        if m:
                            add_ffn(ht, m - 1)
                        else:
                            add_ffn(ht - 1, CHUNKS - 1)
                    dve.wait_ge(g_hi_done, M + 1)
                    low(g_lo[:, m % 2, :], gate[:, :], g_hi[:, m % 2, :].bitcast(f32), g_split)
                    if not last and m:
                        merge(ht + 1, m - 1)
                    if not last and m == CHUNKS - 1:
                        split_fw(ht + 1, 1)
                    if not first and m == 0:
                        split_fw(ht, 2)
                    if last and m:
                        layer_norm(CHUNKS + m - 1, m - 1)
            hidden_tiles(dve, ffn_body)
            add_ffn(HT - 1, CHUNKS - 1)
            layer_norm(2 * CHUNKS - 1, CHUNKS - 1)


def _tables():
    half = HEAD // 2
    inv = np.power(np.float32(THETA), -np.arange(half, dtype=np.float32) / np.float32(half)).astype(np.float32)
    angle = np.arange(SEQ, dtype=np.float32)[None, :] * inv[:, None]
    cos, sin = np.cos(angle).astype(np.float32), np.sin(angle).astype(np.float32)
    rope = np.stack([np.concatenate([cos, cos]), np.concatenate([-sin, sin])], axis=1)
    slot, query = np.arange(P)[None, :], np.arange(P)[:, None]
    return np.ascontiguousarray(rope), (slot > query).astype(np.int32), np.eye(P, dtype=np.float32)


def kernel(L0_attn_x, L0_attn_wq, L0_attn_wk, L0_attn_wv, L0_attn_wo, L0_ffn_w1, L0_ffn_w3, L0_ffn_w2,
           L0_ffn_lora_A1, L0_ffn_lora_B1, L0_ffn_lora_A3, L0_ffn_lora_B3, L0_ffn_lora_A2, L0_ffn_lora_B2):
    from concourse import bacc
    from concourse.bass_utils import run_bass_kernel_spmd

    x, wq, wk, wv, wo, w1, w3, w2, a1, b1, a3, b3, a2, b2 = (np.asarray(a) for a in (
        L0_attn_x, L0_attn_wq, L0_attn_wk, L0_attn_wv, L0_attn_wo, L0_ffn_w1, L0_ffn_w3, L0_ffn_w2,
        L0_ffn_lora_A1, L0_ffn_lora_B1, L0_ffn_lora_A3, L0_ffn_lora_B3, L0_ffn_lora_A2, L0_ffn_lora_B2))
    f = x.dtype
    rope, later, ident = _tables()

    x_rows = x.reshape(ALL_BLOCKS, P, DIM).transpose(1, 0, 2)
    x_cols = x.reshape(CHUNKS, CHUNK, KD, P).transpose(0, 3, 2, 1)
    q_pieces = wq.reshape(KD, P, KV_HEADS, GROUP, HEAD).transpose(2, 3, 1, 0, 4)
    k_pieces = wk.reshape(KD, P, KV_HEADS, 1, HEAD).transpose(2, 3, 1, 0, 4)
    v_pieces = wv.reshape(KD, P, KV_HEADS, 1, HEAD).transpose(2, 3, 1, 0, 4)
    qkv = np.concatenate([q_pieces, k_pieces, v_pieces], axis=1).reshape(KV_HEADS, PROJ, P, CHUNK)
    wo_pieces = wo.reshape(KV_HEADS, GROUP, P, DIM)
    attn_w = np.concatenate([wo_pieces, np.roll(qkv, -1, axis=0)], axis=1).reshape(-1, P, CHUNK)
    pad = HT * P - HIDDEN

    def up_tiles(w):
        w = np.pad(w, ((0, pad), (0, 0)))
        return w.reshape(HT, P, KD, P).transpose(0, 3, 2, 1).reshape(HT, P, CHUNK)

    def hidden_tiles(w):
        return np.pad(w, ((0, pad), (0, 0))).reshape(HT, P, -1)

    ffn_w = np.stack([up_tiles(w1), up_tiles(w3), hidden_tiles(w2.T)], axis=1).reshape(-1, P, CHUNK)
    lora_tile = np.stack([hidden_tiles(b1).transpose(0, 2, 1), hidden_tiles(b3).transpose(0, 2, 1),
                          hidden_tiles(a2.T).transpose(0, 2, 1)], axis=2)
    lora_all = np.stack([a1, a3, b2.T], axis=1)

    arrays = {"x_rows": x_rows, "x_cols": x_cols, "attn_w": attn_w, "rope": rope, "later": later, "ident": ident,
              "ffn_w": ffn_w, "lora_tile": lora_tile, "lora_all": lora_all}
    arrays = {k: np.ascontiguousarray(v) for k, v in arrays.items()}
    nc = bacc.Bacc("TRN2", target_bir_lowering=False, num_devices=1)
    args = [nc.dram_tensor(k, v.shape, mybir.dt.from_np(v.dtype), kind="ExternalInput").ap() for k, v in arrays.items()]
    out = nc.dram_tensor("out", (P, ALL_BLOCKS, DIM), mybir.dt.from_np(np.dtype(f)), kind="ExternalOutput").ap()
    attention_and_ffn(nc, *args, out)
    got = run_bass_kernel_spmd(nc, [arrays], core_ids=[0]).results[0]["out"]
    return np.asarray(got).transpose(1, 0, 2).reshape(BATCH, SEQ, DIM)
```

```python
from contextlib import ExitStack

import numpy as np
import concourse.bass as bass
from concourse import mybir

BATCH, SEQ, DIM = 2, 1024, 512
HEAD = 128
Q_HEADS, KV_HEADS = 32, 8
GROUP = Q_HEADS // KV_HEADS
THETA = 10000.0
HIDDEN, RANK = 1376, 16
EPS = 1e-5
LORA_SCALE = 2.0

P = 128
KD = DIM // P
CHUNK = 512
BPC = CHUNK // P
BLOCKS = SEQ // P
ALL_BLOCKS = BATCH * BLOCKS
CHUNKS = BATCH * SEQ // CHUNK
ITERS = BATCH * KV_HEADS
PIECES = 10
WO_PIECES = GROUP
PROJ = PIECES - WO_PIECES
K_PROJ, V_PROJ = 4, 5
ROPES = 5
RING = 5
HT = -(-HIDDEN // P)
NEG = float(np.finfo(np.float32).min)

EARLY = [0, 1, 3, K_PROJ]
LATE = [(2, 0), (2, 1), (V_PROJ, 0), (V_PROJ, 1)]
SUB = P // GROUP
SUBS = P // SUB
KEYS = P + SUB
PAIR = 2
SPLITS = {1: [0, 1, 2, 3], 2: [4, 5], 3: [6], 4: [7, 8], 5: [9]}

FIRST_NORMS = [list(range(c * BPC, (c + 1) * BPC)) for c in range(CHUNKS)]
NORMS = FIRST_NORMS + FIRST_NORMS[:-1] + [FIRST_NORMS[-1][:-1], FIRST_NORMS[-1][-1:]]
NORMED = [sum(map(len, NORMS[:c])) for c in range(len(NORMS) + 1)]
NORM_AT = {(KV_HEADS, 3): 0, (KV_HEADS, 7): 1, (ITERS - 1, 5): 2}
TAIL_TURNS = {(4, 0): [0], (4, 1): [1], (5, 0): [2], (5, 1): [3], (6, 0): [4], (6, 1): [5], (7, 0): [6], (7, 1): [7]}
TAIL_ADAPTERS = {(5, 0): 0, (5, 1): 1, (6, 0): 2}
FFN_TURNS = {(0, 0): [8], (0, 1): [9], (0, 2): [10], (1, 0): [11], (1, 1): [12], (1, 2): [13], (2, 0): [14], (2, 1): [15]}


def attention_and_ffn(nc, x_rows, x_cols, attn_w, rope, outside, merging, ident, ffn_w, lora_tile, lora_all, out):
    f32, f32r, i32 = mybir.dt.float32, mybir.dt.float32r, mybir.dt.int32
    ALU, ACT, AX = mybir.AluOpType, mybir.ActivationFunctionType, mybir.AxisListType
    SCALE = float(HEAD) ** -0.5

    ctx = ExitStack()
    attn_ctx = ExitStack()
    proj_ctx = ExitStack()
    with ctx:
        def sb(where, name, shape, dt=f32):
            return where.enter_context(nc.sbuf_tensor(name, shape, dt))

        def sem(name):
            return ctx.enter_context(nc.semaphore(name))

        def bank(name, banks=1):
            return ctx.enter_context(nc.psum_tensor(name, [P, CHUNK * banks], f32))

        rows = sb(ctx, "rows", [P, ALL_BLOCKS, DIM])
        x_hi = sb(ctx, "x_hi", [P, 2, KD, CHUNK], f32r)
        x_lo = sb(ctx, "x_lo", [P, 2, KD, CHUNK], f32r)
        id_sb = sb(ctx, "id_sb", [P, P])
        stats = sb(ctx, "stats", [P, BPC, 6])
        moments = sb(ctx, "moments", [P, BPC, 2])
        var_eps = sb(ctx, "var_eps", [P, BPC])
        minus_half = sb(ctx, "minus_half", [P, BPC])
        rstd0 = sb(ctx, "rstd0", [P, BPC])
        newton = sb(ctx, "newton", [P, 3, BPC])
        rstd = sb(ctx, "rstd", [P, BPC])

        start = nc.sbuf_bytes_remaining
        w_raw = sb(attn_ctx, "w_raw", [P, RING, CHUNK])
        wo_hi = sb(attn_ctx, "wo_hi", [P, WO_PIECES, CHUNK], f32r)
        wo_lo = sb(attn_ctx, "wo_lo", [P, WO_PIECES, CHUNK], f32r)
        outside_sb = sb(attn_ctx, "outside_sb", [P, SUBS, P], i32)
        merging_sb = sb(attn_ctx, "merging_sb", [P, PAIR, SUB], i32)
        none_before = sb(attn_ctx, "none_before", [P, P])
        q_rot = sb(attn_ctx, "q_rot", [P, 2, BPC * SUBS, GROUP, SUB])
        k_rot = sb(attn_ctx, "k_rot", [P, SEQ])
        v_cols = sb(attn_ctx, "v_cols", [P, CHUNK])
        v_hi = sb(attn_ctx, "v_hi", [P, BLOCKS, HEAD], f32r)
        v_lo = sb(attn_ctx, "v_lo", [P, BLOCKS, HEAD], f32r)
        neg_max = sb(attn_ctx, "neg_max", [P, SUBS])
        exp_bias = sb(attn_ctx, "exp_bias", [P, SUBS])
        sums = sb(attn_ctx, "sums", [P, SUBS])
        inv_sums = sb(attn_ctx, "inv_sums", [P, SUBS])
        probs = sb(attn_ctx, "probs", [P, SUBS, P])
        pt_hi = sb(attn_ctx, "pt_hi", [P, GROUP, P])
        pt_lo = sb(attn_ctx, "pt_lo", [P, GROUP, P])
        masked = sb(attn_ctx, "masked", [P, 4, CHUNK], f32r)
        o_hi = sb(attn_ctx, "o_hi", [P, CHUNK], f32r)
        o_lo = sb(attn_ctx, "o_lo", [P, CHUNK], f32r)
        attn_bytes = start - nc.sbuf_bytes_remaining
        attn_ctx.close()

        start = nc.sbuf_bytes_remaining
        y_hi = sb(ctx, "y_hi", [P, 2, KD, CHUNK], f32r)
        y_lo = sb(ctx, "y_lo", [P, 2, KD, CHUNK], f32r)
        silu = sb(ctx, "silu", [P, CHUNK])
        gate = sb(ctx, "gate", [P, CHUNK])
        g_hi = sb(ctx, "g_hi", [P, 2, CHUNK], f32r)
        g_lo = sb(ctx, "g_lo", [P, 2, CHUNK], f32r)
        left = attn_bytes - (start - nc.sbuf_bytes_remaining)
        sb(ctx, "rest", [P, left // 4])

        x_raw = sb(proj_ctx, "x_raw", [P, KD, CHUNK])
        w_hi = sb(proj_ctx, "w_hi", [P, PROJ, CHUNK], f32r)
        w_lo = sb(proj_ctx, "w_lo", [P, PROJ, CHUNK], f32r)
        cos_sin = sb(proj_ctx, "cos_sin", [P, 2, SEQ])
        swapped = sb(proj_ctx, "swapped", [P, 2, CHUNK])
        by_cos = sb(proj_ctx, "by_cos", [P, CHUNK])
        proj_ctx.close()

        ffn_raw = sb(ctx, "ffn_raw", [P, 3, CHUNK])
        merged = sb(ctx, "merged", [P, 3, CHUNK])
        fw_hi = sb(ctx, "fw_hi", [P, 3, CHUNK], f32r)
        fw_lo = sb(ctx, "fw_lo", [P, 3, CHUNK], f32r)
        lora_sb = sb(ctx, "lora_sb", [RANK, 3, P])
        lora_full = sb(ctx, "lora_full", [RANK, 3, DIM])

        ps_proj = [bank("ps_proj0"), bank("ps_proj1")]
        ps_scores = bank("ps_scores", 2)
        ps_pt, ps_o, ps_out, ps_v = bank("ps_pt"), bank("ps_o"), bank("ps_out"), bank("ps_v")
        ps_h1, ps_h3 = ps_proj
        down_banks = [ps_scores[:, 0:CHUNK], ps_scores[:, CHUNK:2 * CHUNK], ps_o[:, :], ps_out[:, :]]
        scores = ps_scores[:, :].rearrange("p (a c) -> p a c", a=SUBS // PAIR)
        pt_by_head = ps_pt[:, :].rearrange("p (s h q) -> p h s q", s=SUBS, h=GROUP)

        x_loaded, rows_loaded, rope_loaded = [sem(f"x_loaded{k}") for k in range(KD)], sem("rows_loaded"), sem("rope_loaded")
        w_loaded = [sem(f"w_loaded{r}") for r in range(RING)]
        consts_loaded, const_set = sem("consts_loaded"), sem("const_set")
        x_hi_done, x_split = sem("x_hi_done"), sem("x_split")
        w_hi_done, w_split = sem("w_hi_done"), sem("w_split")
        proj_done, v_turned, scores_done, pt_done = sem("proj_done"), sem("v_turned"), sem("scores_done"), sem("pt_done")
        pv_done, out_done = sem("pv_done"), sem("out_done")
        halves_swapped, by_cos_done, by_sin_done, rotated = sem("halves_swapped"), sem("by_cos_done"), sem("by_sin_done"), sem("rotated")
        v_copied, v_hi_done, v_split = sem("v_copied"), sem("v_hi_done"), sem("v_split")
        row_merged, max_done, bias_done, exp_done = sem("row_merged"), sem("max_done"), sem("bias_done"), sem("exp_done")
        inv_done, probs_done = sem("inv_done"), sem("probs_done")
        pt_hi_done, pt_split, masks_done = sem("pt_hi_done"), sem("pt_split"), sem("masks_done")
        o_hi_done, o_split, rows_added = sem("o_hi_done"), sem("o_split"), sem("rows_added")
        stats_done, moments_done, var_done, pow_done = sem("stats_done"), sem("moments_done"), sem("var_done"), sem("pow_done")
        newton_done, normed = sem("newton_done"), sem("normed")
        y_turned, y_hi_done, y_split = sem("y_turned"), sem("y_hi_done"), sem("y_split")
        ffn_loaded = [sem(f"ffn_loaded{p}") for p in range(3)]
        lora_loaded, lora_done, merge_done = sem("lora_loaded"), sem("lora_done"), sem("merge_done")
        fw_hi_done, fw_split = sem("fw_hi_done"), sem("fw_split")
        h1_done, h3_done, silu_done, gate_done, g_hi_done, g_split = (
            sem("h1_done"), sem("h3_done"), sem("silu_done"), sem("gate_done"), sem("g_hi_done"), sem("g_split"))
        down_done, ffn_added, stored = sem("down_done"), sem("ffn_added"), sem("stored")

        def iterations(eng, body):
            body(0, 0, True, False)
            with eng.Fori(1, KV_HEADS - 1) as i:
                body(i, 0, False, False)
            body(KV_HEADS - 1, 0, False, False)
            body(KV_HEADS, 1, False, False)
            with eng.Fori(KV_HEADS + 1, ITERS - 1) as i:
                body(i, 1, False, False)
            body(ITERS - 1, 1, False, True)

        def hidden_tiles(eng, body):
            body(0, True, False)
            with eng.Fori(1, HT - 1) as ht:
                body(ht, False, False)
            body(HT - 1, False, True)

        def next_chunk(I, j):
            return 2 * I + 1 + j // BPC

        def piece_number(I, p):
            return PROJ + PIECES * I + p

        def normed_columns(m):
            return (x_hi[:, m], x_lo[:, m]) if m < 2 else (y_hi[:, m - 2], y_lo[:, m - 2])

        def proj_bank(C, p):
            return ps_proj[p % 2 if isinstance(C, int) and C == 0 else p in (LATE[0][0], V_PROJ)]

        def turn_bank(b):
            return ps_proj[1] if b < BLOCKS else ps_v

        def late_done(j):
            p, half = LATE[j % BPC]
            return p if half else None

        def slot_major(v):
            return v.rearrange("p h (s q) -> p h s q", s=SUBS)

        def adapter_bank(ht):
            return ps_proj[0] if isinstance(ht, int) and ht == 0 else ps_pt

        block = ctx.enter_context(nc.Block())

        @block.sync
        def _(sp):
            def load_x(c):
                for k in range(KD):
                    if c:
                        sp.wait_ge(x_split, KD * (c - 1) + k + 1)
                    sp.dma_start(x_raw[:, k, :], x_cols[c, :, k, :]).then_inc(x_loaded[k], 16)

            def load_w(I, p, row):
                number = piece_number(I, p)
                sp.wait_ge(w_split, number - RING + 1)
                sp.dma_start(w_raw[:, (PROJ + p) % RING, :], attn_w[row]).then_inc(w_loaded[(PROJ + p) % RING], 16)

            first_row = PIECES * (KV_HEADS - 1) + WO_PIECES
            sp.dma_start(w_raw[:, 0, :], attn_w[first_row]).then_inc(w_loaded[0], 16)
            load_x(0)
            for p in range(1, RING):
                sp.dma_start(w_raw[:, p, :], attn_w[first_row + p]).then_inc(w_loaded[p], 16)
            sp.dma_start(cos_sin[:, :, :], rope).then_inc(rope_loaded, 16)
            sp.dma_start(id_sb[:, :], ident).then_inc(consts_loaded, 16)
            sp.dma_start(outside_sb[:, :, :], outside).then_inc(consts_loaded, 16)
            sp.dma_start(merging_sb[:, :, :], merging).then_inc(consts_loaded, 16)
            sp.wait_ge(w_split, 1)
            sp.dma_start(w_raw[:, 0, :], attn_w[first_row + RING]).then_inc(w_loaded[0], 16)
            load_x(1)
            sp.dma_start(rows[:, :, :], x_rows).then_inc(rows_loaded, 16)
            load_x(2)

            def body(I, batch, first, last):
                for p in range(WO_PIECES if last else PIECES):
                    load_w(I, p, PIECES * (I - KV_HEADS * batch) + p)
                if not isinstance(I, int):
                    return
                if I == KV_HEADS - 1:
                    load_x(3)
            iterations(sp, body)

            sp.wait_ge(rotated, ROPES * 2 * ITERS)
            sp.wait_ge(v_copied, 2 * ITERS)
            sp.dma_start(lora_full[:, :, :], lora_all).then_inc(lora_loaded, 16)
            sp.dma_start(lora_sb[:, :, :], lora_tile[0]).then_inc(lora_loaded, 16)
            for p in range(3):
                sp.dma_start(ffn_raw[:, p, :], ffn_w[p]).then_inc(ffn_loaded[p], 16)

            def ffn_body(ht, first, last):
                if last:
                    return
                for p in range(3):
                    sp.wait_ge(merge_done, 3 * ht + p + 1)
                    sp.dma_start(ffn_raw[:, p, :], ffn_w[3 * (ht + 1) + p]).then_inc(ffn_loaded[p], 16)
                sp.dma_start(lora_sb[:, :, :], lora_tile[ht + 1]).then_inc(lora_loaded, 16)
            hidden_tiles(sp, ffn_body)
            for c in range(CHUNKS, len(NORMS)):
                sp.wait_ge(normed, NORMED[c + 1])
                blocks = slice(NORMS[c][0], NORMS[c][-1] + 1)
                sp.dma_start(out[:, blocks, :], rows[:, blocks, :]).then_inc(stored, 16)
            sp.wait_ge(stored, 16 * (len(NORMS) - CHUNKS))

        @block.tensor
        def _(pe):
            def three(out_, a, b, start, stop):
                pe.matmul(out_, a[0], b[0], start=start, stop=False)
                pe.matmul(out_, a[0], b[1], start=False, stop=False)
                return pe.matmul(out_, a[1], b[0], start=False, stop=stop)

            def project(I, C, parity, p, half=None):
                if half != 1:
                    pe.wait_ge(w_split, PIECES * I + p + 1)
                    if isinstance(C, int) and C == 0:
                        if p >= 2:
                            pe.wait_ge(by_cos_done, p - 1)
                    elif p == LATE[0][0]:
                        pe.wait_ge(v_copied, C)
                    else:
                        pe.wait_ge(by_cos_done, ROPES * C + {0: 0, 1: 1, 3: 2, K_PROJ: 4, V_PROJ: 3}[p])
                for k in {None: range(KD), 0: range(KD // 2), 1: range(KD // 2, KD)}[half]:
                    if isinstance(C, int) and C == 0 and p == 0:
                        pe.wait_ge(x_split, k + 1)
                    cols = slice(k * P, (k + 1) * P)
                    mm = three(proj_bank(C, p)[:, :], (w_hi[:, p, cols], w_lo[:, p, cols]),
                               (x_hi[:, parity, k, :], x_lo[:, parity, k, :]), k == 0, k == KD - 1)
                if half != 0:
                    mm.then_inc(proj_done, 1)

            def turn_v(C):
                pe.wait_ge(v_copied, C + 1)
                if not (isinstance(C, int) and C == 0):
                    pe.wait_ge(v_split, C)
                for t in range(BPC):
                    mm = pe.transpose(ps_v[:, t * P:(t + 1) * P], v_cols[:, t * P:(t + 1) * P], id_sb[:, :])
                mm.then_inc(v_turned, 1)

            def score(n, j):
                c = (j // BPC) % 2
                pe.wait_ge(rotated, ROPES * (n // BPC + 1) if isinstance(n, int) else ROPES * chunk_of[0] + ROPES)
                if not (isinstance(n, int) and n == 0):
                    pe.wait_ge(exp_done, n)
                for s in range(SUBS):
                    q = q_rot[:, c, SUBS * (j % BPC) + s, :, :].rearrange("p h q -> p (h q)")
                    a, b = divmod(s, PAIR)
                    if j == 0:
                        mm = pe.matmul(scores[:, a, b * (KEYS + SUB):b * (KEYS + SUB) + P], q, k_rot[:, 0:P],
                                       start=True, stop=True)
                    else:
                        first_key = (j - 1) * P + s * SUB
                        mm = pe.matmul(scores[:, a, b * KEYS:(b + 1) * KEYS], q, k_rot[:, first_key:first_key + KEYS],
                                       start=True, stop=True)
                mm.then_inc(scores_done, 1)

            def turn_probs(n):
                pe.wait_ge(probs_done, n + 1)
                if not (isinstance(n, int) and n == 0):
                    pe.wait_ge(pt_split, n)
                for s in range(SUBS):
                    mm = pe.transpose(ps_pt[:, s * P:(s + 1) * P], probs[:, s, :], id_sb[:, :])
                mm.then_inc(pt_done, 1)

            def values(n, j):
                pe.wait_ge(masks_done, 4 * (n + 1))
                if j % BPC == 0:
                    pe.wait_ge(v_split, chunk_of[0] + 1)
                if not (isinstance(n, int) and n == 0):
                    pe.wait_ge(o_split, n)
                if j:
                    three(ps_o[:, :], (v_hi[:, j - 1, :], v_lo[:, j - 1, :]), (masked[:, 1, :], masked[:, 3, :]), True, False)
                three(ps_o[:, :], (v_hi[:, j, :], v_lo[:, j, :]), (masked[:, 0, :], masked[:, 2, :]), j == 0, True)\
                    .then_inc(pv_done, 1)

            def output(n, I):
                pe.wait_ge(o_split, n + 1)
                if not (isinstance(n, int) and n == 0):
                    pe.wait_ge(rows_added, n)
                for h in range(GROUP):
                    pe.wait_ge(w_split, piece_number(I, h + 1))
                    cols = slice(h * P, (h + 1) * P)
                    mm = three(ps_out[:, :], (o_hi[:, cols], o_lo[:, cols]), (wo_hi[:, h, :], wo_lo[:, h, :]),
                               h == 0, h == GROUP - 1)
                mm.then_inc(out_done, 1)

            def adapter(ht, p):
                number = 3 * ht + p
                first = isinstance(ht, int) and ht == 0
                ps = adapter_bank(ht)
                if p == 0:
                    pe.wait_ge(lora_loaded, 16 * (ht + 2))
                if not (first and p == 0):
                    pe.wait_ge(merge_done, number)
                if p < 2:
                    for k in range(KD):
                        mm = pe.matmul(ps[:, k * P:(k + 1) * P], lora_full[:, p, k * P:(k + 1) * P],
                                       lora_sb[:, p, :], start=True, stop=True)
                else:
                    mm = pe.matmul(ps[:, :], lora_sb[:, 2, :], lora_full[:, 2, :], start=True, stop=True)
                mm.then_inc(lora_done, 1)

            def turn(blocks):
                for b in blocks:
                    pe.wait_ge(normed, b + 1)
                    if b:
                        pe.wait_ge(y_split, b)
                    else:
                        pe.wait_ge(v_copied, 2 * ITERS)
                    for k in range(KD):
                        mm = pe.transpose(turn_bank(b)[:, k * P:(k + 1) * P], rows[:, b, k * P:(k + 1) * P], id_sb[:, :])
                    mm.then_inc(y_turned, 1)

            def up(ht, m, p, ps, done):
                M = CHUNKS * ht + m
                pe.wait_ge(fw_split, 3 * ht + p + 1)
                if not (isinstance(M, int) and M == 0):
                    pe.wait_ge(gate_done if p else silu_done, M)
                hi, lo = normed_columns(m)
                for k in range(KD):
                    cols = slice(k * P, (k + 1) * P)
                    mm = three(ps[:, :], (fw_hi[:, p, cols], fw_lo[:, p, cols]), (hi[:, k, :], lo[:, k, :]),
                               k == 0, k == KD - 1)
                mm.then_inc(done, 1)

            def down(ht, m):
                M = CHUNKS * ht + m
                pe.wait_ge(fw_split, 3 * ht + 3)
                pe.wait_ge(g_split, M + 1)
                for t in range(BPC):
                    if not (isinstance(M, int) and M == 0):
                        pe.wait_ge(ffn_added, BPC * (M - 1) + t + 1)
                    cols = slice(t * P, (t + 1) * P)
                    three(down_banks[t], (g_hi[:, m % 2, cols], g_lo[:, m % 2, cols]),
                          (fw_hi[:, 2, :], fw_lo[:, 2, :]), True, True).then_inc(down_done, 1)

            chunk_of = [0]

            def fill(j, late):
                turn(TAIL_TURNS[j, late])
                if (j, late) in TAIL_ADAPTERS:
                    adapter(0, TAIL_ADAPTERS[j, late])

            for p in range(PROJ):
                project(0, 0, 0, p)
            pe.wait_ge(consts_loaded, 48)

            def body(I, batch, first, last):
                for j in range(BLOCKS):
                    n = BLOCKS * I + j
                    C = next_chunk(I, j)
                    early = EARLY[j % BPC]
                    weights_of = I + j // BPC
                    projects = not (last and j >= BPC)
                    if projects:
                        if batch == 0 and isinstance(I, int) and j % BPC == 0:
                            if first and j == 0:
                                pe.wait_ge(x_split, 2 * KD)
                            if I == KV_HEADS - 1 and j == BPC:
                                pe.wait_ge(x_split, 3 * KD)
                        if batch == 1 and j == 0:
                            pe.wait_ge(x_split, 4 * KD)
                        project(weights_of, C, (j // BPC + 1) % 2, early)
                    else:
                        fill(j, 0)
                    if not (first and j == 0):
                        turn_probs(n - 1)
                    chunk_of[0] = 2 * I + j // BPC
                    score(n, j)
                    if j % BPC == 0:
                        turn_v(2 * I + j // BPC)
                    if not (first and j < 2):
                        output(n - 2, I if j >= 2 else I - 1)
                    if projects:
                        project(weights_of, C, (j // BPC + 1) % 2, *LATE[j % BPC])
                    else:
                        fill(j, 1)
                    if not (first and j == 0):
                        chunk_of[0] = 2 * I + (j - 1) // BPC
                        values(n - 1, (j - 1) % BLOCKS)
            iterations(pe, body)
            n = BLOCKS * ITERS
            turn_probs(n - 1)
            output(n - 2, ITERS - 1)
            values(n - 1, BLOCKS - 1)
            output(n - 1, ITERS - 1)

            def ffn_body(ht, first, last):
                for m in range(CHUNKS):
                    if first:
                        pe.wait_ge(y_split, max(BLOCKS, BPC * (m + 1)))
                    up(ht, m, 0, ps_h1, h1_done)
                    turn(FFN_TURNS.get((m, 0), []) if first else [])
                    up(ht, m, 1, ps_h3, h3_done)
                    turn(FFN_TURNS.get((m, 1), []) if first else [])
                    if not (first and m == 0):
                        if m:
                            down(ht, m - 1)
                        else:
                            down(ht - 1, CHUNKS - 1)
                    turn(FFN_TURNS.get((m, 2), []) if first else [])
                    if not last and m:
                        adapter(ht + 1, m - 1)
            hidden_tiles(pe, ffn_body)
            down(HT - 1, CHUNKS - 1)

        @block.scalar
        def _(act):
            def split_x(c, k):
                act.wait_ge(x_loaded[k], 16 * (c + 1))
                if c >= 2:
                    act.wait_ge(proj_done, PROJ * (2 * KV_HEADS - 3 + c))
                act.activation(x_hi[:, c % 2, k, :], x_raw[:, k, :], ACT.Copy).then_inc(x_hi_done, 1)

            def split_w(I, p):
                number = piece_number(I, p)
                act.wait_ge(w_loaded[(PROJ + p) % RING], 16 * (2 * I + (PROJ + p) // RING + 1))
                if p < WO_PIECES:
                    if not (isinstance(I, int) and I == 0):
                        act.wait_ge(out_done, BLOCKS * I)
                else:
                    act.wait_ge(proj_done, PROJ * (2 * I + 1) + p - WO_PIECES + 1)
                place = wo_hi[:, p, :] if p < WO_PIECES else w_hi[:, p - WO_PIECES, :]
                act.activation(place, w_raw[:, (PROJ + p) % RING, :], ACT.Copy).then_inc(w_hi_done, 1)

            def swap_halves(C, p):
                act.wait_ge(proj_done, PROJ * C + p + 1)
                if p >= 2:
                    act.wait_ge(rotated, ROPES * C + p - 1)
                elif not (isinstance(C, int) and C == 0):
                    act.wait_ge(rotated, ROPES * C if p == 0 else ROPES * C - 1)
                half = HEAD // 2
                ps = proj_bank(C, p)
                act.activation(swapped[0:half, p % 2, :], ps[half:HEAD, :], ACT.Copy)
                act.activation(swapped[half:HEAD, p % 2, :], ps[0:half, :], ACT.Copy).then_inc(halves_swapped, 1)

            def copy_v(C):
                act.wait_ge(proj_done, PROJ * (C + 1))
                if not (isinstance(C, int) and C == 0):
                    act.wait_ge(v_turned, C)
                act.activation(v_cols[:, :], proj_bank(C, V_PROJ)[:, :], ACT.Copy).then_inc(v_copied, 1)

            def split_v(C, parity):
                act.wait_ge(v_turned, C + 1)
                act.activation(v_hi[:, parity * BPC:(parity + 1) * BPC, :],
                               ps_v[:, :].rearrange("p (t d) -> p t d", t=BPC), ACT.Copy).then_inc(v_hi_done, 1)

            def split_pt(n):
                act.wait_ge(pt_done, n + 1)
                if not (isinstance(n, int) and n == 0):
                    act.wait_ge(masks_done, 4 * n)
                act.activation(slot_major(pt_hi[:, :, :].bitcast(f32r)), pt_by_head, ACT.Copy).then_inc(pt_hi_done, 1)

            def exponentials(n, j):
                act.wait_ge(bias_done, n + 1)
                if not (isinstance(n, int) and n == 0):
                    act.wait_ge(pt_done, n)
                for s in range(SUBS):
                    a, b = divmod(s, PAIR)
                    merged_row = scores[:, a, b * (KEYS + SUB):b * (KEYS + SUB) + P]
                    place = probs[:, s, :]
                    if j and s in (1, 2):
                        merged_row = merged_row.rearrange("p (u c) -> p u c", u=2)[:, ::-1, :]
                        place = place.rearrange("p (u c) -> p u c", u=2)
                    e = act.activation(place, merged_row, ACT.Exp, bias=exp_bias[:, s:s + 1],
                                       scale=SCALE, accum_out=sums[:, s:s + 1])
                e.then_inc(exp_done, 1)

            def split_o(n):
                act.wait_ge(pv_done, n + 1)
                if not (isinstance(n, int) and n == 0):
                    act.wait_ge(out_done, n)
                act.activation(o_hi[:, :], ps_o[:, :], ACT.Copy).then_inc(o_hi_done, 1)

            def first_w(p):
                act.wait_ge(w_loaded[p % RING], 16 * (p // RING + 1))
                act.activation(w_hi[:, p, :], w_raw[:, p % RING, :], ACT.Copy).then_inc(w_hi_done, 1)

            def split_fw(ht, p):
                act.wait_ge(merge_done, 3 * ht + p + 1)
                if not (isinstance(ht, int) and ht == 0):
                    act.wait_ge([h1_done, h3_done, down_done][p], (BPC if p == 2 else 1) * CHUNKS * ht)
                act.activation(fw_hi[:, p, :], merged[:, p, :], ACT.Copy).then_inc(fw_hi_done, 1)

            def split_y(blocks):
                for b in blocks:
                    act.wait_ge(y_turned, b + 1)
                    t = b % BPC
                    act.activation(normed_columns(b // BPC)[0][:, :, t * P:(t + 1) * P],
                                   turn_bank(b)[:, :].rearrange("p (k t) -> p k t", k=KD), ACT.Copy).then_inc(y_hi_done, 1)

            def fill(j, late):
                split_y(TAIL_TURNS[j, late])
                if (j, late) in TAIL_ADAPTERS:
                    split_fw(0, TAIL_ADAPTERS[j, late])

            first_w(0)
            for k in range(KD):
                split_x(0, k)
            for p in range(1, PROJ):
                first_w(p)
            for p in range(ROPES):
                swap_halves(0, p)
            copy_v(0)
            for k in range(KD):
                split_x(1, k)

            def body(I, batch, first, last):
                for j in range(BLOCKS):
                    n = BLOCKS * I + j
                    C = next_chunk(I, j)
                    early, late = EARLY[j % BPC], late_done(j)
                    projects = not (last and j >= BPC)
                    if not projects:
                        fill(j, 0)
                    if not (first and j == 0):
                        split_pt(n - 1)
                    if projects:
                        swap_halves(C, early)
                    exponentials(n, j)
                    if j % BPC == 0:
                        split_v(2 * I + j // BPC, j // BPC)
                    if projects and late == V_PROJ:
                        copy_v(C)
                    elif projects and late is not None:
                        swap_halves(C, late)
                    if not projects:
                        fill(j, 1)
                    if not (first and j == 0):
                        split_o(n - 1)
                    for p in SPLITS.get(j, []):
                        if not (last and p >= WO_PIECES):
                            split_w(I, p)
                    if isinstance(I, int) and I == KV_HEADS - 1:
                        split_x(2 + j // BPC, j % BPC)
            iterations(act, body)
            n = BLOCKS * ITERS
            split_pt(n - 1)
            split_o(n - 1)

            def ffn_body(ht, first, last):
                for m in range(CHUNKS):
                    M = CHUNKS * ht + m
                    act.wait_ge(h1_done, M + 1)
                    if not (first and m == 0):
                        act.wait_ge(gate_done, M)
                    act.activation(silu[:, :], ps_h1[:, :], ACT.Silu).then_inc(silu_done, 1)
                    split_y(FFN_TURNS.get((m, 0), []) if first else [])
                    if not last and m == CHUNKS - 1:
                        split_fw(ht + 1, 0)
                    act.wait_ge(gate_done, M + 1)
                    if not (first and m < 2):
                        act.wait_ge(down_done, BPC * (M - 1))
                    act.activation(g_hi[:, m % 2, :], gate[:, :], ACT.Copy).then_inc(g_hi_done, 1)
                    for after in (1, 2):
                        split_y(FFN_TURNS.get((m, after), []) if first else [])
                    if not last and m == CHUNKS - 1:
                        split_fw(ht + 1, 1)
                    if not first and m == 0:
                        split_fw(ht, 2)
            hidden_tiles(act, ffn_body)

        @block.gpsimd
        def _(pool):
            pool.memset(minus_half[:, :], -0.5).then_inc(const_set, 1)
            pool.wait_ge(rope_loaded, 16)

            def by_sin(C, p, parity):
                pool.wait_ge(halves_swapped, ROPES * C + p + 1)
                pool.tensor_tensor(swapped[:, p % 2, :], swapped[:, p % 2, :],
                                   cos_sin[:, 1, parity * CHUNK:(parity + 1) * CHUNK], ALU.mult).then_inc(by_sin_done, 1)

            def mask(n):
                for part, src, ready in ((0, pt_hi, pt_hi_done), (2, pt_lo, pt_split)):
                    counts = [n, n + 1] if isinstance(n, int) else [pool.to_reg(n), pool.to_reg(n + 1)]
                    pool.wait_ge(const_set, 1)
                    pool.wait_ge(ready, counts[1])
                    if part == 0 and not (isinstance(n, int) and n == 0):
                        pool.wait_ge(pv_done, counts[0])
                    for before in range(2):
                        sign = -1 if before else 1
                        pool.affine_select(
                            out=masked[:, part + before, :].rearrange("p (h q) -> p h q", h=GROUP),
                            in_=src[:, :, :], compare_op=ALU.is_ge, fill=0.0, base=-before,
                            pattern=[[0, GROUP], [sign, P]], channel_multiplier=-sign).then_inc(masks_done, 1)

            def inverse_root(call):
                count = len(NORMS[call])
                pool.wait_ge(var_done, call + 1)
                pool.wait_ge(const_set, 1)
                pool.tensor_tensor(rstd0[:, 0:count], var_eps[:, 0:count], minus_half[:, 0:count], ALU.pow).then_inc(pow_done, 1)

            for p in range(ROPES):
                by_sin(0, p, 0)

            def body(I, batch, first, last):
                for j in range(BLOCKS):
                    n = BLOCKS * I + j
                    C = next_chunk(I, j)
                    early, late = EARLY[j % BPC], late_done(j)
                    projects = not (last and j >= BPC)
                    if not (first and j == 0):
                        mask(n - 1)
                    if projects:
                        by_sin(C, early, (j // BPC + 1) % 2)
                    if projects and late not in (None, V_PROJ):
                        by_sin(C, late, (j // BPC + 1) % 2)
                    if isinstance(I, int) and (I, j) in NORM_AT:
                        inverse_root(NORM_AT[I, j])
            iterations(pool, body)
            mask(BLOCKS * ITERS - 1)
            for call in range(CHUNKS - 1, len(NORMS)):
                inverse_root(call)

        @block.vector
        def _(dve):
            def low(out_, full, hi, done):
                dve.tensor_tensor(out_, full, hi, ALU.subtract).then_inc(done, 1)

            def split_x(c, k):
                dve.wait_ge(x_hi_done, KD * c + k + 1)
                low(x_lo[:, c % 2, k, :], x_raw[:, k, :], x_hi[:, c % 2, k, :].bitcast(f32), x_split)

            def split_w(I, p):
                dve.wait_ge(w_hi_done, piece_number(I, p) + 1)
                hi, lo, at = (wo_hi, wo_lo, p) if p < WO_PIECES else (w_hi, w_lo, p - WO_PIECES)
                low(lo[:, at, :], w_raw[:, (PROJ + p) % RING, :], hi[:, at, :].bitcast(f32), w_split)

            def by_cos_(C, p, parity):
                dve.wait_ge(halves_swapped, ROPES * C + p + 1)
                if not (isinstance(C, int) and C == 0 and p == 0):
                    dve.wait_ge(rotated, ROPES * C + p)
                dve.tensor_tensor(by_cos[:, :], proj_bank(C, p)[:, :],
                                  cos_sin[:, 0, parity * CHUNK:(parity + 1) * CHUNK], ALU.mult).then_inc(by_cos_done, 1)

            def rotate(C, p, parity):
                dve.wait_ge(by_cos_done, ROPES * C + p + 1)
                dve.wait_ge(by_sin_done, ROPES * C + p + 1)
                if not (isinstance(C, int) and C < 2):
                    dve.wait_ge(scores_done, BPC * (C - 1) + (p == K_PROJ))
                if p == K_PROJ:
                    place, parts = k_rot[:, parity * CHUNK:(parity + 1) * CHUNK], (by_cos[:, :], swapped[:, p % 2, :])
                else:
                    place = q_rot[:, parity, :, p, :]
                    parts = (v.rearrange("p (s q) -> p s q", q=SUB) for v in (by_cos[:, :], swapped[:, p % 2, :]))
                dve.tensor_tensor(place, *parts, ALU.add).then_inc(rotated, 1)

            def split_v(C, parity):
                dve.wait_ge(v_hi_done, C + 1)
                blocks = slice(parity * BPC, (parity + 1) * BPC)
                low(v_lo[:, blocks, :], ps_v[:, :].rearrange("p (t d) -> p t d", t=BPC), v_hi[:, blocks, :].bitcast(f32), v_split)

            def split_pt(n):
                dve.wait_ge(pt_hi_done, n + 1)
                low(slot_major(pt_lo[:, :, :]), pt_by_head, slot_major(pt_hi[:, :, :]), pt_split)

            def both(even, odd, width=SUB):
                at = ps_scores[:, even:even + 1]
                return bass.AP(tensor=at.tensor, offset=at.offset,
                               ap=[list(at.ap[0]), [CHUNK, SUBS // PAIR], [odd - even, PAIR], [1, width]])

            all_rows = both(0, KEYS + SUB, P)

            def row_max(n, j):
                count = n + 1 if isinstance(n, int) else dve.to_reg(n + 1)
                dve.wait_ge(consts_loaded, 48)
                dve.wait_ge(scores_done, count)
                if j:
                    dve.copy_predicated(both(0, KEYS + P), merging_sb[:, :, :].unsqueeze(1).broadcast_to([P, SUBS // PAIR, PAIR, SUB]),
                                        both(P, KEYS)).then_inc(row_merged, 1)
                else:
                    dve.copy_predicated(all_rows, outside_sb[:, :, :].rearrange("p (a b) c -> p a b c", b=PAIR),
                                        none_before[:, :].unsqueeze(1).unsqueeze(1).broadcast_to([P, SUBS // PAIR, PAIR, P])
                                        ).then_inc(row_merged, 1)
                dve.wait_ge(row_merged, n + 1)
                dve.tensor_reduce(neg_max[:, :].rearrange("p (a b) -> p a b", b=PAIR), all_rows, AX.X, ALU.max,
                                  negate=True).then_inc(max_done, 1)
                dve.wait_ge(max_done, n + 1)
                dve.tensor_scalar(exp_bias[:, :], neg_max[:, :], SCALE, None, ALU.mult).then_inc(bias_done, 1)

            def normalise(n):
                dve.wait_ge(exp_done, n + 1)
                dve.reciprocal(inv_sums[:, :], sums[:, :]).then_inc(inv_done, 1)
                dve.wait_ge(inv_done, n + 1)
                dve.tensor_tensor(probs[:, :, :], probs[:, :, :], inv_sums[:, :].unsqueeze(2).broadcast_to([P, SUBS, P]),
                                  ALU.mult).then_inc(probs_done, 1)

            def add_rows(n, b):
                dve.wait_ge(out_done, n + 1)
                dve.tensor_tensor(rows[:, b, :], ps_out[:, :], rows[:, b, :], ALU.add).then_inc(rows_added, 1)

            def split_o(n):
                dve.wait_ge(o_hi_done, n + 1)
                low(o_lo[:, :], ps_o[:, :], o_hi[:, :].bitcast(f32), o_split)

            def first_w(p):
                dve.wait_ge(w_hi_done, p + 1)
                low(w_lo[:, p, :], w_raw[:, p % RING, :], w_hi[:, p, :].bitcast(f32), w_split)

            def layer_norm(call):
                blocks, count = NORMS[call], len(NORMS[call])
                for t, b in enumerate(blocks):
                    if call < CHUNKS:
                        dve.wait_ge(rows_added, BLOCKS * (KV_HEADS * (b // BLOCKS + 1) - 1) + b % BLOCKS + 1)
                    else:
                        dve.wait_ge(ffn_added, ALL_BLOCKS * (HT - 1) + b + 1)
                    dve.bn_stats(stats[:, t, :], rows[:, b, :]).then_inc(stats_done, 1)
                for t in range(count):
                    dve.wait_ge(stats_done, NORMED[call] + t + 1)
                    dve.bn_aggr(moments[:, t, :], stats[:, t, :]).then_inc(moments_done, 1)
                dve.wait_ge(moments_done, NORMED[call + 1])
                dve.tensor_scalar(var_eps[:, 0:count], moments[:, 0:count, 1], EPS, None, ALU.add).then_inc(var_done, 1)
                r0, v, r = rstd0[:, 0:count], var_eps[:, 0:count], rstd[:, 0:count]
                a, b_, c = newton[:, 0, 0:count], newton[:, 1, 0:count], newton[:, 2, 0:count]
                dve.wait_ge(pow_done, call + 1)
                dve.tensor_tensor(a, r0, r0, ALU.mult).then_inc(newton_done, 1)
                dve.wait_ge(newton_done, 4 * call + 1)
                dve.tensor_tensor(b_, a, v, ALU.mult).then_inc(newton_done, 1)
                dve.wait_ge(newton_done, 4 * call + 2)
                dve.tensor_scalar(c, b_, -0.5, 1.5, ALU.mult, ALU.add).then_inc(newton_done, 1)
                dve.wait_ge(newton_done, 4 * call + 3)
                dve.tensor_tensor(r, c, r0, ALU.mult).then_inc(newton_done, 1)
                dve.wait_ge(newton_done, 4 * call + 4)
                for t, b in enumerate(blocks):
                    dve.tensor_scalar(rows[:, b, :], rows[:, b, :], moments[:, t, 0:1], rstd[:, t:t + 1],
                                      ALU.subtract, ALU.mult).then_inc(normed, 1)

            def merge(ht, p):
                dve.wait_ge(lora_done, 3 * ht + p + 1)
                dve.wait_ge(ffn_loaded[p], 16 * (ht + 1))
                if not (isinstance(ht, int) and ht == 0):
                    dve.wait_ge(fw_split, 3 * (ht - 1) + p + 1)
                dve.scalar_tensor_tensor(out=merged[:, p, :], in0=adapter_bank(ht)[:, :], scalar=LORA_SCALE,
                                         in1=ffn_raw[:, p, :], op0=ALU.mult, op1=ALU.add).then_inc(merge_done, 1)

            def split_fw(ht, p):
                dve.wait_ge(fw_hi_done, 3 * ht + p + 1)
                low(fw_lo[:, p, :], merged[:, p, :], fw_hi[:, p, :].bitcast(f32), fw_split)

            def split_y(blocks):
                for b in blocks:
                    dve.wait_ge(y_hi_done, b + 1)
                    hi, lo = normed_columns(b // BPC)
                    cols = slice(b % BPC * P, (b % BPC + 1) * P)
                    low(lo[:, :, cols], turn_bank(b)[:, :].rearrange("p (k t) -> p k t", k=KD), hi[:, :, cols].bitcast(f32), y_split)

            def fill(j, late):
                split_y(TAIL_TURNS[j, late])
                if (j, late) in TAIL_ADAPTERS:
                    merge(0, TAIL_ADAPTERS[j, late])
                    split_fw(0, TAIL_ADAPTERS[j, late])

            def add_ffn(ht, m):
                M = CHUNKS * ht + m
                for t in range(BPC):
                    dve.wait_ge(down_done, BPC * M + t + 1)
                    b = BPC * m + t
                    dve.tensor_tensor(rows[:, b, :], down_banks[t], rows[:, b, :], ALU.add).then_inc(ffn_added, 1)

            dve.memset(none_before[:, :], NEG).then_inc(const_set, 1)
            first_w(0)
            for k in range(KD):
                split_x(0, k)
            for p in range(1, PROJ):
                first_w(p)
            dve.wait_ge(rope_loaded, 16)
            dve.wait_ge(const_set, 2)
            for p in range(ROPES):
                by_cos_(0, p, 0)
                rotate(0, p, 0)
            for k in range(KD):
                split_x(1, k)
            dve.wait_ge(rows_loaded, 16)

            def body(I, batch, first, last):
                for j in range(BLOCKS):
                    n = BLOCKS * I + j
                    C = next_chunk(I, j)
                    parity = (j // BPC + 1) % 2
                    early, late = EARLY[j % BPC], late_done(j)
                    projects = not (last and j >= BPC)
                    rotates_late = projects and late not in (None, V_PROJ)
                    if not projects:
                        fill(j, 0)
                    if not (first and j == 0):
                        split_pt(n - 1)
                    if projects:
                        by_cos_(C, early, parity)
                    row_max(n, j)
                    normalise(n)
                    if not (first and j < 2):
                        before = j < 2 and isinstance(I, int) and I == KV_HEADS
                        add_rows(n - 2, BLOCKS * (batch - before) + (j - 2) % BLOCKS)
                    if projects:
                        rotate(C, early, parity)
                    if j % BPC == 0:
                        split_v(2 * I + j // BPC, j // BPC)
                    if rotates_late:
                        by_cos_(C, late, parity)
                    if not projects:
                        fill(j, 1)
                    if not (first and j == 0):
                        split_o(n - 1)
                    for p in SPLITS.get(j, []):
                        if not (last and p >= WO_PIECES):
                            split_w(I, p)
                    if rotates_late:
                        rotate(C, late, parity)
                    if isinstance(I, int) and (I, j) in NORM_AT:
                        layer_norm(NORM_AT[I, j])
                    if isinstance(I, int) and I == KV_HEADS - 1:
                        split_x(2 + j // BPC, j % BPC)
            iterations(dve, body)
            n = BLOCKS * ITERS
            split_pt(n - 1)
            add_rows(n - 2, ALL_BLOCKS - 2)
            split_o(n - 1)
            add_rows(n - 1, ALL_BLOCKS - 1)

            def ffn_body(ht, first, last):
                for m in range(CHUNKS):
                    M = CHUNKS * ht + m
                    split_y(FFN_TURNS.get((m, 0), []) if first else [])
                    if not last and m == CHUNKS - 1:
                        split_fw(ht + 1, 0)
                    dve.wait_ge(silu_done, M + 1)
                    dve.wait_ge(h3_done, M + 1)
                    if not (first and m == 0):
                        dve.wait_ge(g_split, M)
                    dve.tensor_tensor(gate[:, :], ps_h3[:, :], silu[:, :], ALU.mult).then_inc(gate_done, 1)
                    split_y(FFN_TURNS.get((m, 1), []) if first else [])
                    if not (first and m == 0):
                        if m:
                            add_ffn(ht, m - 1)
                        else:
                            add_ffn(ht - 1, CHUNKS - 1)
                    dve.wait_ge(g_hi_done, M + 1)
                    low(g_lo[:, m % 2, :], gate[:, :], g_hi[:, m % 2, :].bitcast(f32), g_split)
                    split_y(FFN_TURNS.get((m, 2), []) if first else [])
                    if first and m == 0:
                        layer_norm(CHUNKS - 1)
                    if not last and m:
                        merge(ht + 1, m - 1)
                    if not last and m == CHUNKS - 1:
                        split_fw(ht + 1, 1)
                    if not first and m == 0:
                        split_fw(ht, 2)
                    if last and m:
                        layer_norm(CHUNKS + m - 1)
            hidden_tiles(dve, ffn_body)
            add_ffn(HT - 1, CHUNKS - 1)
            layer_norm(2 * CHUNKS - 1)
            layer_norm(2 * CHUNKS)


def _tables():
    half = HEAD // 2
    inv = np.power(np.float32(THETA), -np.arange(half, dtype=np.float32) / np.float32(half)).astype(np.float32)
    angle = np.arange(SEQ, dtype=np.float32)[None, :] * inv[:, None]
    cos, sin = np.cos(angle).astype(np.float32), np.sin(angle).astype(np.float32)
    rope = np.stack([np.concatenate([cos, cos]), np.concatenate([-sin, sin])], axis=1)
    sub, slot, query = np.arange(SUBS)[None, :, None], np.arange(P)[None, None, :], (np.arange(P) % SUB)[:, None, None]
    outside = slot > sub * SUB + query
    key = np.arange(SUB)[None, None, :]
    merging = np.concatenate([key <= query, key > query], axis=1)
    return np.ascontiguousarray(rope), outside.astype(np.int32), merging.astype(np.int32), np.eye(P, dtype=np.float32)


def kernel(L0_attn_x, L0_attn_wq, L0_attn_wk, L0_attn_wv, L0_attn_wo, L0_ffn_w1, L0_ffn_w3, L0_ffn_w2,
           L0_ffn_lora_A1, L0_ffn_lora_B1, L0_ffn_lora_A3, L0_ffn_lora_B3, L0_ffn_lora_A2, L0_ffn_lora_B2):
    from concourse import bacc
    from concourse.bass_utils import run_bass_kernel_spmd

    x, wq, wk, wv, wo, w1, w3, w2, a1, b1, a3, b3, a2, b2 = (np.asarray(a) for a in (
        L0_attn_x, L0_attn_wq, L0_attn_wk, L0_attn_wv, L0_attn_wo, L0_ffn_w1, L0_ffn_w3, L0_ffn_w2,
        L0_ffn_lora_A1, L0_ffn_lora_B1, L0_ffn_lora_A3, L0_ffn_lora_B3, L0_ffn_lora_A2, L0_ffn_lora_B2))
    f = x.dtype
    rope, outside, merging, ident = _tables()

    x_rows = x.reshape(ALL_BLOCKS, P, DIM).transpose(1, 0, 2)
    x_cols = x.reshape(CHUNKS, CHUNK, KD, P).transpose(0, 3, 2, 1)
    q_pieces = wq.reshape(KD, P, KV_HEADS, GROUP, HEAD).transpose(2, 3, 1, 0, 4)
    k_pieces = wk.reshape(KD, P, KV_HEADS, 1, HEAD).transpose(2, 3, 1, 0, 4)
    v_pieces = wv.reshape(KD, P, KV_HEADS, 1, HEAD).transpose(2, 3, 1, 0, 4)
    qkv = np.concatenate([q_pieces, k_pieces, v_pieces], axis=1).reshape(KV_HEADS, PROJ, P, CHUNK)
    wo_pieces = wo.reshape(KV_HEADS, GROUP, P, DIM)
    attn_w = np.concatenate([wo_pieces, np.roll(qkv, -1, axis=0)], axis=1).reshape(-1, P, CHUNK)
    pad = HT * P - HIDDEN

    def up_tiles(w):
        w = np.pad(w, ((0, pad), (0, 0)))
        return w.reshape(HT, P, KD, P).transpose(0, 3, 2, 1).reshape(HT, P, CHUNK)

    def hidden_tiles(w):
        return np.pad(w, ((0, pad), (0, 0))).reshape(HT, P, -1)

    ffn_w = np.stack([up_tiles(w1), up_tiles(w3), hidden_tiles(w2.T)], axis=1).reshape(-1, P, CHUNK)
    lora_tile = np.stack([hidden_tiles(b1).transpose(0, 2, 1), hidden_tiles(b3).transpose(0, 2, 1),
                          hidden_tiles(a2.T).transpose(0, 2, 1)], axis=2)
    lora_all = np.stack([a1, a3, b2.T], axis=1)

    arrays = {"x_rows": x_rows, "x_cols": x_cols, "attn_w": attn_w, "rope": rope, "outside": outside, "merging": merging, "ident": ident,
              "ffn_w": ffn_w, "lora_tile": lora_tile, "lora_all": lora_all}
    arrays = {k: np.ascontiguousarray(v) for k, v in arrays.items()}
    nc = bacc.Bacc("TRN2", target_bir_lowering=False, num_devices=1)
    args = [nc.dram_tensor(k, v.shape, mybir.dt.from_np(v.dtype), kind="ExternalInput").ap() for k, v in arrays.items()]
    out = nc.dram_tensor("out", (P, ALL_BLOCKS, DIM), mybir.dt.from_np(np.dtype(f)), kind="ExternalOutput").ap()
    attention_and_ffn(nc, *args, out)
    got = run_bass_kernel_spmd(nc, [arrays], core_ids=[0]).results[0]["out"]
    return np.asarray(got).transpose(1, 0, 2).reshape(BATCH, SEQ, DIM)
```

```python
from contextlib import ExitStack

import numpy as np
import concourse.bass as bass
from concourse import mybir

BATCH, SEQ, DIM = 2, 1024, 512
HEAD = 128
Q_HEADS, KV_HEADS = 32, 8
GROUP = Q_HEADS // KV_HEADS
THETA = 10000.0
HIDDEN, RANK = 1376, 16
EPS = 1e-5
LORA_SCALE = 2.0
SECTION = 32

P = 128
KD = DIM // P
CHUNK = 512
BPC = CHUNK // P
BLOCKS = SEQ // P
ALL_BLOCKS = BATCH * BLOCKS
CHUNKS = BATCH * SEQ // CHUNK
ITERS = BATCH * KV_HEADS
PIECES = 10
WO_PIECES = GROUP
PROJ = PIECES - WO_PIECES
K_PROJ, V_PROJ = 4, 5
ROPES = 5
RING = 5
HT = -(-HIDDEN // P)
NEG = float(np.finfo(np.float32).min)

EARLY = [0, 1, 3, K_PROJ]
LATE = [(2, 0), (2, 1), (V_PROJ, 0), (V_PROJ, 1)]
SUB = P // GROUP
SUBS = P // SUB
KEYS = P + SUB
PAIR = 2
SPLITS = {1: [0, 1, 2, 3], 2: [4, 5], 3: [6], 4: [7, 8], 5: [9]}

STATS_AT = {(KV_HEADS, 0): [(0, 0), (0, 1)], (KV_HEADS, 1): [(0, 2), (0, 3)],
            (KV_HEADS, 3): [(1, 0), (1, 1)], (KV_HEADS, 4): [(1, 2), (1, 3)],
            (ITERS - 1, 2): [(2, 0)], (ITERS - 1, 3): [(2, 1)], (ITERS - 1, 4): [(2, 2)], (ITERS - 1, 5): [(2, 3)],
            (ITERS - 1, 6): [(3, 0)], (ITERS - 1, 7): [(3, 1)]}
FACTORS_AT = {(KV_HEADS, 2): 0, (KV_HEADS, 5): 1, (ITERS - 1, 6): 2}
TAIL_TURNS = {(4, 0): [0], (4, 1): [], (5, 0): [1, 2], (5, 1): [3], (6, 0): [4], (6, 1): [5], (7, 0): [6], (7, 1): [7]}
TAIL_ADAPTERS = {5: 0, 6: 1, 7: 2}
FFN_TURNS = {(0, 1): [8], (0, 2): [9], (1, 0): [10, 11], (1, 1): [12], (1, 2): [13], (2, 0): [14], (2, 1): [15]}
SPARE_TURNS = (9, 11)


def attention_and_ffn(nc, x_rows, x_cols, attn_w, rope, outside, merging, ident, ffn_w, lora_a, lora_b, lora_a2, lora_b2, out):
    f32, f32r, i32 = mybir.dt.float32, mybir.dt.float32r, mybir.dt.int32
    ALU, ACT, AX = mybir.AluOpType, mybir.ActivationFunctionType, mybir.AxisListType
    SCALE = float(HEAD) ** -0.5

    ctx = ExitStack()
    attn_ctx = ExitStack()
    proj_ctx = ExitStack()
    with ctx:
        def sb(where, name, shape, dt=f32):
            return where.enter_context(nc.sbuf_tensor(name, shape, dt))

        def sem(name):
            return ctx.enter_context(nc.semaphore(name))

        def bank(name, banks=1):
            return ctx.enter_context(nc.psum_tensor(name, [P, CHUNK * banks], f32))

        rows = sb(ctx, "rows", [P, ALL_BLOCKS, DIM])
        x_hi = sb(ctx, "x_hi", [P, 2, KD, CHUNK], f32r)
        x_lo = sb(ctx, "x_lo", [P, 2, KD, CHUNK], f32r)
        id_sb = sb(ctx, "id_sb", [P, P])
        stats = sb(ctx, "stats", [P, BPC, 6])
        moments = sb(ctx, "moments", [P, BPC, 2])
        var_eps = sb(ctx, "var_eps", [P, BPC])
        minus_half = sb(ctx, "minus_half", [P, BPC])
        rstd0 = sb(ctx, "rstd0", [P, BPC])
        newton = sb(ctx, "newton", [P, 3, BPC])
        rstd = sb(ctx, "rstd", [P, 2, BPC])
        neg_mean = sb(ctx, "neg_mean", [P, 2, BPC])

        start = nc.sbuf_bytes_remaining
        w_raw = sb(attn_ctx, "w_raw", [P, RING, CHUNK])
        wo_hi = sb(attn_ctx, "wo_hi", [P, WO_PIECES, CHUNK], f32r)
        wo_lo = sb(attn_ctx, "wo_lo", [P, WO_PIECES, CHUNK], f32r)
        outside_sb = sb(attn_ctx, "outside_sb", [P, SUBS, P], i32)
        merging_sb = sb(attn_ctx, "merging_sb", [P, PAIR, SUB], i32)
        none_before = sb(attn_ctx, "none_before", [P, P])
        q_rot = sb(attn_ctx, "q_rot", [P, 2, BPC * SUBS, GROUP, SUB])
        k_rot = sb(attn_ctx, "k_rot", [P, SEQ])
        v_cols = sb(attn_ctx, "v_cols", [P, CHUNK])
        v_hi = sb(attn_ctx, "v_hi", [P, BLOCKS, HEAD], f32r)
        v_lo = sb(attn_ctx, "v_lo", [P, BLOCKS, HEAD], f32r)
        neg_max = sb(attn_ctx, "neg_max", [P, SUBS])
        exp_bias = sb(attn_ctx, "exp_bias", [P, SUBS])
        sums = sb(attn_ctx, "sums", [P, SUBS])
        inv_sums = sb(attn_ctx, "inv_sums", [P, SUBS])
        probs = sb(attn_ctx, "probs", [P, SUBS, P])
        pt_hi = sb(attn_ctx, "pt_hi", [P, GROUP, P])
        pt_lo = sb(attn_ctx, "pt_lo", [P, GROUP, P])
        masked = sb(attn_ctx, "masked", [P, 4, CHUNK], f32r)
        o_hi = sb(attn_ctx, "o_hi", [P, CHUNK], f32r)
        o_lo = sb(attn_ctx, "o_lo", [P, CHUNK], f32r)
        attn_bytes = start - nc.sbuf_bytes_remaining
        attn_ctx.close()

        start = nc.sbuf_bytes_remaining
        y_hi = sb(ctx, "y_hi", [P, 2, KD, CHUNK], f32r)
        y_lo = sb(ctx, "y_lo", [P, 2, KD, CHUNK], f32r)
        silu = sb(ctx, "silu", [P, CHUNK])
        gate = sb(ctx, "gate", [P, CHUNK])
        last_hi = sb(ctx, "last_hi", [P, 3, CHUNK], f32r)
        last_lo = sb(ctx, "last_lo", [P, 3, CHUNK], f32r)
        g_hi = sb(ctx, "g_hi", [P, 2, CHUNK], f32r)
        g_lo = sb(ctx, "g_lo", [P, 2, CHUNK], f32r)
        left = attn_bytes - (start - nc.sbuf_bytes_remaining)
        sb(ctx, "rest", [P, left // 4])

        x_raw = sb(proj_ctx, "x_raw", [P, KD, CHUNK])
        w_hi = sb(proj_ctx, "w_hi", [P, PROJ, CHUNK], f32r)
        w_lo = sb(proj_ctx, "w_lo", [P, PROJ, CHUNK], f32r)
        cos_sin = sb(proj_ctx, "cos_sin", [P, 2, SEQ])
        swapped = sb(proj_ctx, "swapped", [P, 2, CHUNK])
        by_cos = sb(proj_ctx, "by_cos", [P, CHUNK])
        proj_ctx.close()

        ffn_raw = sb(ctx, "ffn_raw", [P, 3, CHUNK])
        merged = sb(ctx, "merged", [P, 3, CHUNK])
        fw_hi = sb(ctx, "fw_hi", [P, 3, CHUNK], f32r)
        fw_lo = sb(ctx, "fw_lo", [P, 3, CHUNK], f32r)
        a_raw = sb(ctx, "a_raw", [P, 2, P])
        a_stack = sb(ctx, "a_stack", [P, 2, P], f32r)
        b_raw = sb(ctx, "b_raw", [P, 2, CHUNK])
        b_hi = sb(ctx, "b_hi", [P, 2, CHUNK], f32r)
        b_lo = sb(ctx, "b_lo", [P // 2, 2, CHUNK], f32r)
        a2_raw = sb(ctx, "a2_raw", [3 * SECTION, P])
        a2_stack = sb(ctx, "a2_stack", [3 * SECTION, P], f32r)
        b2_raw = sb(ctx, "b2_raw", [3 * SECTION, DIM])
        b2_stack = sb(ctx, "b2_stack", [3 * SECTION, DIM], f32r)

        ps_proj = [bank("ps_proj0"), bank("ps_proj1")]
        ps_scores = bank("ps_scores", 2)
        ps_pt, ps_o, ps_out, ps_v = bank("ps_pt"), bank("ps_o"), bank("ps_out"), bank("ps_v")
        ps_h1, ps_h3 = ps_proj
        down_banks = [ps_scores[:, 0:CHUNK], ps_scores[:, CHUNK:2 * CHUNK], ps_o[:, :], ps_out[:, :]]
        scores = ps_scores[:, :].rearrange("p (a c) -> p a c", a=SUBS // PAIR)
        pt_by_head = ps_pt[:, :].rearrange("p (s h q) -> p h s q", s=SUBS, h=GROUP)

        x_loaded = [sem(f"x_loaded{k}") for k in range(KD)]
        rows_loaded, rope_loaded = [sem(f"rows_loaded{b}") for b in range(BATCH)], [sem(f"rope_loaded{h}") for h in range(2)]
        w_loaded = [sem(f"w_loaded{r}") for r in range(RING)]
        ident_loaded, rules_loaded, const_set = sem("ident_loaded"), sem("rules_loaded"), sem("const_set")
        x_hi_done, x_split = sem("x_hi_done"), sem("x_split")
        w_hi_done, w_split = sem("w_hi_done"), sem("w_split")
        proj_done, v_turned, scores_done, pt_done = sem("proj_done"), sem("v_turned"), sem("scores_done"), sem("pt_done")
        pv_done, out_done = sem("pv_done"), sem("out_done")
        halves_swapped, by_cos_done, by_sin_done, rotated = sem("halves_swapped"), sem("by_cos_done"), sem("by_sin_done"), sem("rotated")
        v_copied, v_hi_done, v_split = sem("v_copied"), sem("v_hi_done"), sem("v_split")
        row_merged, max_done, bias_done, exp_done = sem("row_merged"), sem("max_done"), sem("bias_done"), sem("exp_done")
        inv_done, probs_done = sem("inv_done"), sem("probs_done")
        pt_hi_done, pt_split, masks_done = sem("pt_hi_done"), sem("pt_split"), sem("masks_done")
        o_hi_done, o_split, rows_added = sem("o_hi_done"), sem("o_split"), sem("rows_added")
        stats_done, moments_done, var_done, pow_done = sem("stats_done"), sem("moments_done"), sem("var_done"), sem("pow_done")
        newton_done, factors_done = sem("newton_done"), sem("factors_done")
        normed, last_normed = sem("normed"), sem("last_normed")
        y_turned, y_hi_done, y_split = sem("y_turned"), sem("y_hi_done"), sem("y_split")
        ffn_loaded = [sem(f"ffn_loaded{p}") for p in range(3)]
        lora_kept_loaded, lora_kept_hi_done, lora_kept_split = sem("lora_kept_loaded"), sem("lora_kept_hi_done"), sem("lora_kept_split")
        lora_loaded, lora_hi_done, lora_split = sem("lora_loaded"), sem("lora_hi_done"), sem("lora_split")
        lora_done, merge_done = sem("lora_done"), sem("merge_done")
        fw_hi_done, fw_split, last_hi_done, last_split = sem("fw_hi_done"), sem("fw_split"), sem("last_hi_done"), sem("last_split")
        h1_done, h3_done, silu_done, gate_done, g_hi_done, g_split = (
            sem("h1_done"), sem("h3_done"), sem("silu_done"), sem("gate_done"), sem("g_hi_done"), sem("g_split"))
        down_done, ffn_added, stored = sem("down_done"), sem("ffn_added"), sem("stored")

        def iterations(eng, body):
            body(0, 0, True, False)
            with eng.Fori(1, KV_HEADS - 1) as i:
                body(i, 0, False, False)
            body(KV_HEADS - 1, 0, False, False)
            body(KV_HEADS, 1, False, False)
            with eng.Fori(KV_HEADS + 1, ITERS - 1) as i:
                body(i, 1, False, False)
            body(ITERS - 1, 1, False, True)

        def hidden_tiles(eng, body):
            body(0, True)
            with eng.Fori(1, HT - 2) as ht:
                body(ht, False)

        PAIR_STEP = CHUNKS * (HT - 2)
        PAIR_ADDED = ALL_BLOCKS * (HT - 2)
        pair_steps = [(m, u) for m in range(CHUNKS) for u in range(2)]

        def fw(ht):
            return (last_hi, last_lo) if isinstance(ht, int) and ht == HT - 1 else (fw_hi, fw_lo)

        def wait_fw_split(eng, ht, p):
            if isinstance(ht, int) and ht == HT - 1:
                eng.wait_ge(last_split, p + 1)
            else:
                eng.wait_ge(fw_split, 3 * ht + p + 1)

        def next_chunk(I, j):
            return 2 * I + 1 + j // BPC

        def piece_number(I, p):
            return PROJ + PIECES * I + p

        def normed_columns(m):
            return (x_hi[:, m], x_lo[:, m]) if m < 2 else (y_hi[:, m - 2], y_lo[:, m - 2])

        def proj_bank(C, p):
            return ps_proj[p % 2 if isinstance(C, int) and C == 0 else p in (LATE[0][0], V_PROJ)]

        def turn_bank(b):
            return ps_proj[1] if b < BLOCKS and b % 2 == 0 else ps_pt if b in SPARE_TURNS else ps_v

        def late_done(j):
            p, half = LATE[j % BPC]
            return p if half else None

        def slot_major(v):
            return v.rearrange("p h (s q) -> p h s q", s=SUBS)

        def adapter_bank(ht):
            return ps_proj[0] if isinstance(ht, int) and ht == 0 else ps_pt

        block = ctx.enter_context(nc.Block())

        @block.sync
        def _(sp):
            def load_x(c):
                for k in range(KD):
                    if c:
                        sp.wait_ge(x_split, KD * (c - 1) + k + 1)
                    sp.dma_start(x_raw[:, k, :], x_cols[c, :, k, :]).then_inc(x_loaded[k], 16)

            def load_w(I, p, row):
                number = piece_number(I, p)
                sp.wait_ge(w_split, number - RING + 1)
                sp.dma_start(w_raw[:, (PROJ + p) % RING, :], attn_w[row]).then_inc(w_loaded[(PROJ + p) % RING], 16)

            first_row = PIECES * (KV_HEADS - 1) + WO_PIECES
            sp.dma_start(w_raw[:, 0, :], attn_w[first_row]).then_inc(w_loaded[0], 16)
            load_x(0)
            for p in range(1, RING):
                sp.dma_start(w_raw[:, p, :], attn_w[first_row + p]).then_inc(w_loaded[p], 16)
                if p == 1:
                    sp.dma_start(cos_sin[:, :, 0:CHUNK], rope[:, :, 0:CHUNK]).then_inc(rope_loaded[0], 16)
            sp.wait_ge(w_split, 1)
            sp.dma_start(w_raw[:, 0, :], attn_w[first_row + RING]).then_inc(w_loaded[0], 16)
            sp.dma_start(id_sb[:, :], ident).then_inc(ident_loaded, 16)
            load_x(1)
            sp.dma_start(outside_sb[:, :, :], outside).then_inc(rules_loaded, 16)
            sp.dma_start(merging_sb[:, :, :], merging).then_inc(rules_loaded, 16)
            sp.dma_start(cos_sin[:, :, CHUNK:SEQ], rope[:, :, CHUNK:SEQ]).then_inc(rope_loaded[1], 16)
            sp.dma_start(rows[:, 0:BLOCKS, :], x_rows[:, 0:BLOCKS, :]).then_inc(rows_loaded[0], 16)
            load_x(2)

            def body(I, batch, first, last):
                for p in range(WO_PIECES if last else PIECES):
                    load_w(I, p, PIECES * (I - KV_HEADS * batch) + p)
                if not isinstance(I, int):
                    return
                if I == KV_HEADS - 1:
                    load_x(3)
                if I == 0:
                    sp.dma_start(rows[:, BLOCKS:, :], x_rows[:, BLOCKS:, :]).then_inc(rows_loaded[1], 16)
            iterations(sp, body)

            sp.wait_ge(rotated, ROPES * 2 * ITERS)
            sp.wait_ge(v_copied, 2 * ITERS)
            sp.dma_start(a_raw[:, :, :], lora_a).then_inc(lora_kept_loaded, 16)
            sp.dma_start(b2_raw[:, :], lora_b2).then_inc(lora_kept_loaded, 16)
            sp.dma_start(b_raw[:, :, :], lora_b[0]).then_inc(lora_loaded, 16)
            sp.dma_start(a2_raw[:, :], lora_a2[0]).then_inc(lora_loaded, 16)
            for p in range(3):
                sp.dma_start(ffn_raw[:, p, :], ffn_w[p]).then_inc(ffn_loaded[p], 16)

            def load_next(ht):
                sp.wait_ge(lora_split, 2 * (ht + 1))
                sp.dma_start(b_raw[:, :, :], lora_b[ht + 1]).then_inc(lora_loaded, 16)
                sp.dma_start(a2_raw[:, :], lora_a2[ht + 1]).then_inc(lora_loaded, 16)
                for p in range(3):
                    sp.wait_ge(merge_done, 3 * ht + p + 1)
                    sp.dma_start(ffn_raw[:, p, :], ffn_w[3 * (ht + 1) + p]).then_inc(ffn_loaded[p], 16)
            load_next(0)
            with sp.Fori(1, HT - 1) as ht:
                load_next(ht)
            parts = [range(c * BPC, (c + 1) * BPC) for c in range(CHUNKS - 1)] + [[b] for b in range(ALL_BLOCKS - BPC, ALL_BLOCKS)]
            for part in parts:
                in_last = part[-1] - (ALL_BLOCKS - BPC // 2)
                if in_last < 0:
                    sp.wait_ge(normed, ALL_BLOCKS + part[-1] + 1)
                else:
                    sp.wait_ge(last_normed, in_last + 1)
                blocks = slice(part[0], part[-1] + 1)
                sp.dma_start(out[:, blocks, :], rows[:, blocks, :]).then_inc(stored, 16)
            sp.wait_ge(stored, 16 * len(parts))

        @block.tensor
        def _(pe):
            def three(out_, a, b, start, stop):
                pe.matmul(out_, a[0], b[0], start=start, stop=False)
                pe.matmul(out_, a[0], b[1], start=False, stop=False)
                return pe.matmul(out_, a[1], b[0], start=False, stop=stop)

            def project(I, C, parity, p, half=None):
                if half != 1:
                    pe.wait_ge(w_split, PIECES * I + p + 1)
                    if isinstance(C, int) and C == 0:
                        if p >= 2:
                            pe.wait_ge(by_cos_done, p - 1)
                    elif p == LATE[0][0]:
                        pe.wait_ge(v_copied, C)
                    else:
                        pe.wait_ge(by_cos_done, ROPES * C + {0: 0, 1: 1, 3: 2, K_PROJ: 4, V_PROJ: 3}[p])
                for k in {None: range(KD), 0: range(KD // 2), 1: range(KD // 2, KD)}[half]:
                    if isinstance(C, int) and C < 2 and p == 0:
                        pe.wait_ge(x_split, KD * C + k + 1)
                    cols = slice(k * P, (k + 1) * P)
                    mm = three(proj_bank(C, p)[:, :], (w_hi[:, p, cols], w_lo[:, p, cols]),
                               (x_hi[:, parity, k, :], x_lo[:, parity, k, :]), k == 0, k == KD - 1)
                if half != 0:
                    mm.then_inc(proj_done, 1)

            def turn_v(C):
                pe.wait_ge(v_copied, C + 1)
                if not (isinstance(C, int) and C == 0):
                    pe.wait_ge(v_split, C)
                for t in range(BPC):
                    mm = pe.transpose(ps_v[:, t * P:(t + 1) * P], v_cols[:, t * P:(t + 1) * P], id_sb[:, :])
                mm.then_inc(v_turned, 1)

            def score(n, j):
                c = (j // BPC) % 2
                pe.wait_ge(rotated, ROPES * (n // BPC + 1) if isinstance(n, int) else ROPES * chunk_of[0] + ROPES)
                if not (isinstance(n, int) and n == 0):
                    pe.wait_ge(exp_done, n)
                for s in range(SUBS):
                    q = q_rot[:, c, SUBS * (j % BPC) + s, :, :].rearrange("p h q -> p (h q)")
                    a, b = divmod(s, PAIR)
                    if j == 0:
                        mm = pe.matmul(scores[:, a, b * (KEYS + SUB):b * (KEYS + SUB) + P], q, k_rot[:, 0:P],
                                       start=True, stop=True)
                    else:
                        first_key = (j - 1) * P + s * SUB
                        mm = pe.matmul(scores[:, a, b * KEYS:(b + 1) * KEYS], q, k_rot[:, first_key:first_key + KEYS],
                                       start=True, stop=True)
                mm.then_inc(scores_done, 1)

            def turn_probs(n):
                pe.wait_ge(probs_done, n + 1)
                if not (isinstance(n, int) and n == 0):
                    pe.wait_ge(pt_split, n)
                for s in range(SUBS):
                    mm = pe.transpose(ps_pt[:, s * P:(s + 1) * P], probs[:, s, :], id_sb[:, :])
                mm.then_inc(pt_done, 1)

            def values(n, j):
                pe.wait_ge(masks_done, 4 * (n + 1))
                if j % BPC == 0:
                    pe.wait_ge(v_split, chunk_of[0] + 1)
                if not (isinstance(n, int) and n == 0):
                    pe.wait_ge(o_split, n)
                if j:
                    three(ps_o[:, :], (v_hi[:, j - 1, :], v_lo[:, j - 1, :]), (masked[:, 1, :], masked[:, 3, :]), True, False)
                three(ps_o[:, :], (v_hi[:, j, :], v_lo[:, j, :]), (masked[:, 0, :], masked[:, 2, :]), j == 0, True)\
                    .then_inc(pv_done, 1)

            def output(n, I):
                pe.wait_ge(o_split, n + 1)
                if not (isinstance(n, int) and n == 0):
                    pe.wait_ge(rows_added, n)
                for h in range(GROUP):
                    pe.wait_ge(w_split, piece_number(I, h + 1))
                    cols = slice(h * P, (h + 1) * P)
                    mm = three(ps_out[:, :], (o_hi[:, cols], o_lo[:, cols]), (wo_hi[:, h, :], wo_lo[:, h, :]),
                               h == 0, h == GROUP - 1)
                mm.then_inc(out_done, 1)

            def adapter(ht, p):
                number = 3 * ht + p
                first = isinstance(ht, int) and ht == 0
                ps = adapter_bank(ht)
                pe.wait_ge(lora_split, 2 * ht + (2 if p == 2 else 1))
                if first and p == 0:
                    pe.wait_ge(lora_kept_split, 2)
                if not (first and p == 0):
                    pe.wait_ge(merge_done, number)
                if isinstance(ht, int) and ht == 1 and p == 0:
                    pe.wait_ge(y_split, max(SPARE_TURNS) + 1)
                if p < 2:
                    pe.matmul(ps[:, :], a_stack[:, p, :], b_hi[:, p, :], start=True, stop=False)
                    mm = pe.matmul(ps[:, :], a_stack[0:P // 2, p, :], b_lo[:, p, :], start=False, stop=True)
                else:
                    mm = pe.matmul(ps[:, :], a2_stack[:, :], b2_stack[:, :], start=True, stop=True)
                mm.then_inc(lora_done, 1)

            def turn(blocks):
                for b in blocks:
                    pe.wait_ge(normed, b + 1)
                    if b == 0:
                        pe.wait_ge(v_copied, 2 * ITERS)
                    elif b == 1:
                        pe.wait_ge(v_split, 2 * ITERS)
                    else:
                        pe.wait_ge(y_split, b - 1 if b < BLOCKS or b in SPARE_TURNS else b)
                    for k in range(KD):
                        mm = pe.transpose(turn_bank(b)[:, k * P:(k + 1) * P], rows[:, b, k * P:(k + 1) * P], id_sb[:, :])
                    mm.then_inc(y_turned, 1)

            def up(ht, step, m, p):
                wait_fw_split(pe, ht, p)
                if not (isinstance(step, int) and step == 0):
                    pe.wait_ge([silu_done, gate_done][p], step)
                (hi, lo), (w_hi_, w_lo_) = normed_columns(m), fw(ht)
                for k in range(KD):
                    cols = slice(k * P, (k + 1) * P)
                    mm = three([ps_h1, ps_h3][p][:, :], (w_hi_[:, p, cols], w_lo_[:, p, cols]), (hi[:, k, :], lo[:, k, :]),
                               k == 0, k == KD - 1)
                mm.then_inc([h1_done, h3_done][p], 1)

            def down(ht, step, parity, added, start=True, stop=True):
                wait_fw_split(pe, ht, 2)
                pe.wait_ge(g_split, step + 1)
                w_hi_, w_lo_ = fw(ht)
                for t in range(BPC):
                    if added is not None:
                        pe.wait_ge(ffn_added, added + t + 1)
                    cols = slice(t * P, (t + 1) * P)
                    three(down_banks[t], (g_hi[:, parity, cols], g_lo[:, parity, cols]),
                          (w_hi_[:, 2, :], w_lo_[:, 2, :]), start, stop).then_inc(down_done, 1)

            def down_before(ht, m):
                step = CHUNKS * ht + m - 1
                starts = isinstance(step, int) and step == 0
                down(ht if m else ht - 1, step, (m - 1) % 2, None if starts else BPC * (step - 1))

            chunk_of = [0]

            def fill(j, late):
                if late and j in TAIL_ADAPTERS:
                    adapter(0, TAIL_ADAPTERS[j])
                turn(TAIL_TURNS[j, late])

            for p in range(PROJ):
                project(0, 0, 0, p)
            pe.wait_ge(ident_loaded, 16)

            def body(I, batch, first, last):
                for j in range(BLOCKS):
                    n = BLOCKS * I + j
                    C = next_chunk(I, j)
                    early = EARLY[j % BPC]
                    weights_of = I + j // BPC
                    projects = not (last and j >= BPC)
                    if projects:
                        if batch == 0 and isinstance(I, int) and j % BPC == 0:
                            if I == KV_HEADS - 1 and j == BPC:
                                pe.wait_ge(x_split, 3 * KD)
                        if batch == 1 and j == 0:
                            pe.wait_ge(x_split, 4 * KD)
                        project(weights_of, C, (j // BPC + 1) % 2, early)
                    else:
                        fill(j, 0)
                    if not (first and j == 0):
                        turn_probs(n - 1)
                    chunk_of[0] = 2 * I + j // BPC
                    score(n, j)
                    if j % BPC == 0:
                        turn_v(2 * I + j // BPC)
                    if not (first and j < 2):
                        output(n - 2, I if j >= 2 else I - 1)
                    if projects:
                        project(weights_of, C, (j // BPC + 1) % 2, *LATE[j % BPC])
                    else:
                        fill(j, 1)
                    if not (first and j == 0):
                        chunk_of[0] = 2 * I + (j - 1) // BPC
                        values(n - 1, (j - 1) % BLOCKS)
            iterations(pe, body)
            n = BLOCKS * ITERS
            turn_probs(n - 1)
            pe.wait_ge(y_split, BPC)
            pe.wait_ge(merge_done, 3)
            up(0, 0, 0, 0)
            output(n - 2, ITERS - 1)
            values(n - 1, BLOCKS - 1)
            pe.wait_ge(y_split, BLOCKS - 1)
            up(0, 0, 0, 1)
            output(n - 1, ITERS - 1)

            def ffn_body(ht, first):
                for m in range(CHUNKS):
                    step = CHUNKS * ht + m
                    done = first and m == 0
                    if first and m:
                        pe.wait_ge(y_split, BPC * (m + 1))
                    if not done:
                        up(ht, step, m, 0)
                    turn(FFN_TURNS.get((m, 0), []) if first else [])
                    if not done:
                        up(ht, step, m, 1)
                    turn(FFN_TURNS.get((m, 1), []) if first else [])
                    if not done:
                        down_before(ht, m)
                    turn(FFN_TURNS.get((m, 2), []) if first else [])
                    if m:
                        adapter(ht + 1, m - 1)
            hidden_tiles(pe, ffn_body)

            for m, u in pair_steps:
                ht, step = HT - 2 + u, PAIR_STEP + 2 * m + u
                up(ht, step, m, 0)
                if m == 0:
                    adapter(HT - 1, 2 if u else 0)
                up(ht, step, m, 1)
                if (m, u) == (0, 0):
                    adapter(HT - 1, 1)
                    down_before(HT - 2, 0)
                elif u:
                    down(HT - 2, step - 1, 0, PAIR_ADDED + BPC * (m - 1), stop=False)
                else:
                    down(HT - 1, step - 1, 1, None, start=False)
            down(HT - 1, step, 1, None, start=False)

        @block.scalar
        def _(act):
            def split_x(c, k):
                act.wait_ge(x_loaded[k], 16 * (c + 1))
                if c >= 2:
                    act.wait_ge(proj_done, PROJ * (2 * KV_HEADS - 3 + c))
                act.activation(x_hi[:, c % 2, k, :], x_raw[:, k, :], ACT.Copy).then_inc(x_hi_done, 1)

            def split_w(I, p):
                number = piece_number(I, p)
                act.wait_ge(w_loaded[(PROJ + p) % RING], 16 * (2 * I + (PROJ + p) // RING + 1))
                if p < WO_PIECES:
                    if not (isinstance(I, int) and I == 0):
                        act.wait_ge(out_done, BLOCKS * I)
                else:
                    act.wait_ge(proj_done, PROJ * (2 * I + 1) + p - WO_PIECES + 1)
                place = wo_hi[:, p, :] if p < WO_PIECES else w_hi[:, p - WO_PIECES, :]
                act.activation(place, w_raw[:, (PROJ + p) % RING, :], ACT.Copy).then_inc(w_hi_done, 1)

            def swap_halves(C, p):
                act.wait_ge(proj_done, PROJ * C + p + 1)
                if p >= 2:
                    act.wait_ge(rotated, ROPES * C + p - 1)
                elif not (isinstance(C, int) and C == 0):
                    act.wait_ge(rotated, ROPES * C if p == 0 else ROPES * C - 1)
                half = HEAD // 2
                ps = proj_bank(C, p)
                act.activation(swapped[0:half, p % 2, :], ps[half:HEAD, :], ACT.Copy)
                act.activation(swapped[half:HEAD, p % 2, :], ps[0:half, :], ACT.Copy).then_inc(halves_swapped, 1)

            def copy_v(C):
                act.wait_ge(proj_done, PROJ * (C + 1))
                if not (isinstance(C, int) and C == 0):
                    act.wait_ge(v_turned, C)
                act.activation(v_cols[:, :], proj_bank(C, V_PROJ)[:, :], ACT.Copy).then_inc(v_copied, 1)

            def split_v(C, parity):
                act.wait_ge(v_turned, C + 1)
                act.activation(v_hi[:, parity * BPC:(parity + 1) * BPC, :],
                               ps_v[:, :].rearrange("p (t d) -> p t d", t=BPC), ACT.Copy).then_inc(v_hi_done, 1)

            def split_pt(n):
                act.wait_ge(pt_done, n + 1)
                if not (isinstance(n, int) and n == 0):
                    act.wait_ge(masks_done, 4 * n)
                act.activation(slot_major(pt_hi[:, :, :].bitcast(f32r)), pt_by_head, ACT.Copy).then_inc(pt_hi_done, 1)

            def exponentials(n, j):
                act.wait_ge(bias_done, n + 1)
                if not (isinstance(n, int) and n == 0):
                    act.wait_ge(pt_done, n)
                for s in range(SUBS):
                    a, b = divmod(s, PAIR)
                    merged_row = scores[:, a, b * (KEYS + SUB):b * (KEYS + SUB) + P]
                    place = probs[:, s, :]
                    if j and s in (1, 2):
                        merged_row = merged_row.rearrange("p (u c) -> p u c", u=2)[:, ::-1, :]
                        place = place.rearrange("p (u c) -> p u c", u=2)
                    e = act.activation(place, merged_row, ACT.Exp, bias=exp_bias[:, s:s + 1],
                                       scale=SCALE, accum_out=sums[:, s:s + 1])
                e.then_inc(exp_done, 1)

            def split_o(n):
                act.wait_ge(pv_done, n + 1)
                if not (isinstance(n, int) and n == 0):
                    act.wait_ge(out_done, n)
                act.activation(o_hi[:, :], ps_o[:, :], ACT.Copy).then_inc(o_hi_done, 1)

            def first_w(p):
                act.wait_ge(w_loaded[p % RING], 16 * (p // RING + 1))
                act.activation(w_hi[:, p, :], w_raw[:, p % RING, :], ACT.Copy).then_inc(w_hi_done, 1)

            def norm_rows(call, ts=range(BPC)):
                act.wait_ge(factors_done, call + 1)
                for t in ts:
                    b = call % CHUNKS * BPC + t
                    act.activation(rows[:, b, :], rows[:, b, :], ACT.Identity, bias=neg_mean[:, call % 2, t:t + 1],
                                   scale=rstd[:, call % 2, t:t + 1]).then_inc(normed, 1)

            def split_fw(ht, p):
                act.wait_ge(merge_done, 3 * ht + p + 1)
                if isinstance(ht, int) and ht == HT - 1:
                    act.activation(last_hi[:, p, :], merged[:, p, :], ACT.Copy).then_inc(last_hi_done, 1)
                    return
                if not (isinstance(ht, int) and ht == 0):
                    act.wait_ge([h1_done, h3_done, down_done][p], (BPC if p == 2 else 1) * CHUNKS * ht)
                act.activation(fw_hi[:, p, :], merged[:, p, :], ACT.Copy).then_inc(fw_hi_done, 1)

            def gate_curve(step):
                act.wait_ge(h1_done, step + 1)
                if not (isinstance(step, int) and step == 0):
                    act.wait_ge(gate_done, step)
                act.activation(silu[:, :], ps_h1[:, :], ACT.Silu).then_inc(silu_done, 1)

            def lora_kept_hi():
                act.wait_ge(lora_kept_loaded, 32)
                act.activation(a_stack[:, :, :], a_raw[:, :, :], ACT.Copy).then_inc(lora_kept_hi_done, 1)
                act.activation(b2_stack[:, :], b2_raw[:, :], ACT.Copy).then_inc(lora_kept_hi_done, 1)

            def lora_hi(ht):
                act.wait_ge(lora_loaded, 32 * (ht + 1))
                if not (isinstance(ht, int) and ht == 0):
                    act.wait_ge(lora_done, 3 * ht)
                act.activation(b_hi[:, :, :], b_raw[:, :, :], ACT.Copy).then_inc(lora_hi_done, 1)
                act.activation(a2_stack[:, :], a2_raw[:, :], ACT.Copy).then_inc(lora_hi_done, 1)

            def split_y(blocks):
                for b in blocks:
                    act.wait_ge(y_turned, b + 1)
                    t = b % BPC
                    act.activation(normed_columns(b // BPC)[0][:, :, t * P:(t + 1) * P],
                                   turn_bank(b)[:, :].rearrange("p (k t) -> p k t", k=KD), ACT.Copy).then_inc(y_hi_done, 1)

            first_w(0)
            for k in range(KD):
                split_x(0, k)
            for p in range(1, RING):
                first_w(p)
            for p in range(ROPES):
                swap_halves(0, p)
                if p == 1:
                    first_w(RING)
                if p in (2, 3):
                    split_x(1, 2 * p - 4)
                    split_x(1, 2 * p - 3)
            copy_v(0)

            def body(I, batch, first, last):
                for j in range(BLOCKS):
                    n = BLOCKS * I + j
                    C = next_chunk(I, j)
                    early, late = EARLY[j % BPC], late_done(j)
                    projects = not (last and j >= BPC)
                    if not (first and j == 0):
                        split_pt(n - 1)
                    if projects:
                        swap_halves(C, early)
                    else:
                        split_y(TAIL_TURNS[j, 0])
                    exponentials(n, j)
                    for half in range(2):
                        if isinstance(I, int) and (I, j - 1 - half) in FACTORS_AT:
                            norm_rows(FACTORS_AT[I, j - 1 - half], range(2 * half, 2 * half + 2))
                    if j % BPC == 0:
                        split_v(2 * I + j // BPC, j // BPC)
                    if projects and late == V_PROJ:
                        copy_v(C)
                    elif projects and late is not None:
                        swap_halves(C, late)
                    if not projects:
                        split_y(TAIL_TURNS[j, 1])
                    if not (first and j == 0):
                        split_o(n - 1)
                    if not projects and j in TAIL_ADAPTERS and j < BLOCKS - 1:
                        split_fw(0, TAIL_ADAPTERS[j])
                    if last and j == BPC:
                        lora_kept_hi()
                        lora_hi(0)
                    for p in SPLITS.get(j, []):
                        if not (last and p >= WO_PIECES):
                            split_w(I, p)
                    if isinstance(I, int) and I == KV_HEADS - 1 and j % BPC < 2:
                        for k in range(KD // 2 * (j % BPC), KD // 2 * (j % BPC + 1)):
                            split_x(2 + j // BPC, k)
            iterations(act, body)
            n = BLOCKS * ITERS
            split_pt(n - 1)
            split_fw(0, 2)
            lora_hi(1)
            gate_curve(0)
            norm_rows(CHUNKS - 2, range(2, 4))
            split_o(n - 1)

            def gate_hi(step, parity):
                act.wait_ge(gate_done, step + 1)
                if not (isinstance(step, int) and step < 2):
                    act.wait_ge(down_done, BPC * (step - 1))
                act.activation(g_hi[:, parity, :], gate[:, :], ACT.Copy).then_inc(g_hi_done, 1)

            def ffn_body(ht, first):
                for m in range(CHUNKS):
                    step = CHUNKS * ht + m
                    if first and m == 0:
                        split_y(FFN_TURNS[0, 1] + FFN_TURNS[0, 2])
                    else:
                        gate_curve(step)
                    split_y(FFN_TURNS.get((m, 0), []) if first else [])
                    if first and m == 1:
                        norm_rows(CHUNKS - 1)
                    if m == CHUNKS - 1:
                        split_fw(ht + 1, 0)
                    gate_hi(step, m % 2)
                    for after in (1, 2):
                        split_y(FFN_TURNS.get((m, after), []) if first and m else [])
                    if m == CHUNKS - 1:
                        split_fw(ht + 1, 1)
                    if not first and m == 0:
                        split_fw(ht, 2)
                        lora_hi(ht + 1)
            hidden_tiles(act, ffn_body)

            lora_hi(HT - 1)
            for m, u in pair_steps:
                step = PAIR_STEP + 2 * m + u
                gate_curve(step)
                if step == PAIR_STEP:
                    split_fw(HT - 1, 0)
                gate_hi(step, u)
                if step == PAIR_STEP:
                    split_fw(HT - 1, 1)
                    split_fw(HT - 2, 2)
                if step == PAIR_STEP + 1:
                    split_fw(HT - 1, 2)
                if m and u:
                    norm_rows(CHUNKS + m - 1)
            norm_rows(2 * CHUNKS - 1, range(BPC // 2))

        @block.gpsimd
        def _(pool):
            pool.memset(minus_half[:, :], -0.5).then_inc(const_set, 1)
            pool.wait_ge(rope_loaded[0], 16)

            def by_sin(C, p, parity):
                pool.wait_ge(halves_swapped, ROPES * C + p + 1)
                pool.tensor_tensor(swapped[:, p % 2, :], swapped[:, p % 2, :],
                                   cos_sin[:, 1, parity * CHUNK:(parity + 1) * CHUNK], ALU.mult).then_inc(by_sin_done, 1)

            def mask(n):
                for part, src, ready in ((0, pt_hi, pt_hi_done), (2, pt_lo, pt_split)):
                    counts = [n, n + 1] if isinstance(n, int) else [pool.to_reg(n), pool.to_reg(n + 1)]
                    pool.wait_ge(const_set, 1)
                    pool.wait_ge(ready, counts[1])
                    if part == 0 and not (isinstance(n, int) and n == 0):
                        pool.wait_ge(pv_done, counts[0])
                    for before in range(2):
                        sign = -1 if before else 1
                        pool.affine_select(
                            out=masked[:, part + before, :].rearrange("p (h q) -> p h q", h=GROUP),
                            in_=src[:, :, :], compare_op=ALU.is_ge, fill=0.0, base=-before,
                            pattern=[[0, GROUP], [sign, P]], channel_multiplier=-sign).then_inc(masks_done, 1)

            def inverse_root(call):
                pool.wait_ge(var_done, call + 1)
                pool.wait_ge(const_set, 1)
                pool.tensor_tensor(rstd0[:, :], var_eps[:, :], minus_half[:, :], ALU.pow).then_inc(pow_done, 1)

            for p in range(ROPES):
                by_sin(0, p, 0)
            pool.wait_ge(rope_loaded[1], 16)

            def body(I, batch, first, last):
                for j in range(BLOCKS):
                    n = BLOCKS * I + j
                    C = next_chunk(I, j)
                    early, late = EARLY[j % BPC], late_done(j)
                    projects = not (last and j >= BPC)
                    if not (first and j == 0):
                        mask(n - 1)
                    if isinstance(I, int) and (I, j) in FACTORS_AT:
                        inverse_root(FACTORS_AT[I, j])
                    if projects:
                        by_sin(C, early, (j // BPC + 1) % 2)
                    if projects and late not in (None, V_PROJ):
                        by_sin(C, late, (j // BPC + 1) % 2)
            iterations(pool, body)
            mask(BLOCKS * ITERS - 1)
            for call in range(CHUNKS - 1, 2 * CHUNKS):
                inverse_root(call)

        @block.vector
        def _(dve):
            def low(out_, full, hi, done):
                dve.tensor_tensor(out_, full, hi, ALU.subtract).then_inc(done, 1)

            def split_x(c, k):
                dve.wait_ge(x_hi_done, KD * c + k + 1)
                low(x_lo[:, c % 2, k, :], x_raw[:, k, :], x_hi[:, c % 2, k, :].bitcast(f32), x_split)

            def split_w(I, p):
                dve.wait_ge(w_hi_done, piece_number(I, p) + 1)
                hi, lo, at = (wo_hi, wo_lo, p) if p < WO_PIECES else (w_hi, w_lo, p - WO_PIECES)
                low(lo[:, at, :], w_raw[:, (PROJ + p) % RING, :], hi[:, at, :].bitcast(f32), w_split)

            def by_cos_(C, p, parity):
                dve.wait_ge(halves_swapped, ROPES * C + p + 1)
                if not (isinstance(C, int) and C == 0 and p == 0):
                    dve.wait_ge(rotated, ROPES * C + p)
                dve.tensor_tensor(by_cos[:, :], proj_bank(C, p)[:, :],
                                  cos_sin[:, 0, parity * CHUNK:(parity + 1) * CHUNK], ALU.mult).then_inc(by_cos_done, 1)

            def rotate(C, p, parity):
                dve.wait_ge(by_cos_done, ROPES * C + p + 1)
                dve.wait_ge(by_sin_done, ROPES * C + p + 1)
                if not (isinstance(C, int) and C < 2):
                    dve.wait_ge(scores_done, BPC * (C - 1) + (p == K_PROJ))
                if p == K_PROJ:
                    place, parts = k_rot[:, parity * CHUNK:(parity + 1) * CHUNK], (by_cos[:, :], swapped[:, p % 2, :])
                else:
                    place = q_rot[:, parity, :, p, :]
                    parts = (v.rearrange("p (s q) -> p s q", q=SUB) for v in (by_cos[:, :], swapped[:, p % 2, :]))
                dve.tensor_tensor(place, *parts, ALU.add).then_inc(rotated, 1)

            def split_v(C, parity):
                dve.wait_ge(v_hi_done, C + 1)
                blocks = slice(parity * BPC, (parity + 1) * BPC)
                low(v_lo[:, blocks, :], ps_v[:, :].rearrange("p (t d) -> p t d", t=BPC), v_hi[:, blocks, :].bitcast(f32), v_split)

            def split_pt(n):
                dve.wait_ge(pt_hi_done, n + 1)
                low(slot_major(pt_lo[:, :, :]), pt_by_head, slot_major(pt_hi[:, :, :]), pt_split)

            def both(even, odd, width=SUB):
                at = ps_scores[:, even:even + 1]
                return bass.AP(tensor=at.tensor, offset=at.offset,
                               ap=[list(at.ap[0]), [CHUNK, SUBS // PAIR], [odd - even, PAIR], [1, width]])

            all_rows = both(0, KEYS + SUB, P)

            def row_max(n, j):
                count = n + 1 if isinstance(n, int) else dve.to_reg(n + 1)
                dve.wait_ge(rules_loaded, 32)
                dve.wait_ge(scores_done, count)
                if j:
                    dve.copy_predicated(both(0, KEYS + P), merging_sb[:, :, :].unsqueeze(1).broadcast_to([P, SUBS // PAIR, PAIR, SUB]),
                                        both(P, KEYS)).then_inc(row_merged, 1)
                else:
                    dve.copy_predicated(all_rows, outside_sb[:, :, :].rearrange("p (a b) c -> p a b c", b=PAIR),
                                        none_before[:, :].unsqueeze(1).unsqueeze(1).broadcast_to([P, SUBS // PAIR, PAIR, P])
                                        ).then_inc(row_merged, 1)
                dve.wait_ge(row_merged, n + 1)
                dve.tensor_reduce(neg_max[:, :].rearrange("p (a b) -> p a b", b=PAIR), all_rows, AX.X, ALU.max,
                                  negate=True).then_inc(max_done, 1)
                dve.wait_ge(max_done, n + 1)
                dve.tensor_scalar(exp_bias[:, :], neg_max[:, :], SCALE, None, ALU.mult).then_inc(bias_done, 1)

            def normalise(n):
                dve.wait_ge(exp_done, n + 1)
                dve.reciprocal(inv_sums[:, :], sums[:, :]).then_inc(inv_done, 1)
                dve.wait_ge(inv_done, n + 1)
                dve.tensor_tensor(probs[:, :, :], probs[:, :, :], inv_sums[:, :].unsqueeze(2).broadcast_to([P, SUBS, P]),
                                  ALU.mult).then_inc(probs_done, 1)

            def add_rows(n, b):
                dve.wait_ge(out_done, n + 1)
                dve.tensor_tensor(rows[:, b, :], ps_out[:, :], rows[:, b, :], ALU.add).then_inc(rows_added, 1)

            def split_o(n):
                dve.wait_ge(o_hi_done, n + 1)
                low(o_lo[:, :], ps_o[:, :], o_hi[:, :].bitcast(f32), o_split)

            def first_w(p):
                dve.wait_ge(w_hi_done, p + 1)
                low(w_lo[:, p, :], w_raw[:, p % RING, :], w_hi[:, p, :].bitcast(f32), w_split)

            def row_stats(call, t):
                b = call % CHUNKS * BPC + t
                if call < CHUNKS:
                    dve.wait_ge(rows_added, BLOCKS * (KV_HEADS * (b // BLOCKS + 1) - 1) + b % BLOCKS + 1)
                else:
                    dve.wait_ge(ffn_added, PAIR_ADDED + b + 1)
                dve.bn_stats(stats[:, t, :], rows[:, b, :]).then_inc(stats_done, 1)

            def variances(call):
                for t in range(BPC):
                    dve.wait_ge(stats_done, BPC * call + t + 1)
                    dve.bn_aggr(moments[:, t, :], stats[:, t, :]).then_inc(moments_done, 1)
                dve.wait_ge(moments_done, BPC * (call + 1))
                dve.tensor_scalar(var_eps[:, :], moments[:, :, 1], EPS, None, ALU.add).then_inc(var_done, 1)

            def factors(call):
                r = rstd[:, call % 2, :]
                dve.wait_ge(pow_done, call + 1)
                dve.tensor_tensor(newton[:, 0, :], rstd0[:, :], rstd0[:, :], ALU.mult).then_inc(newton_done, 1)
                dve.wait_ge(newton_done, 4 * call + 1)
                dve.tensor_tensor(newton[:, 1, :], newton[:, 0, :], var_eps[:, :], ALU.mult).then_inc(newton_done, 1)
                dve.wait_ge(newton_done, 4 * call + 2)
                dve.tensor_scalar(newton[:, 2, :], newton[:, 1, :], -0.5, 1.5, ALU.mult, ALU.add).then_inc(newton_done, 1)
                dve.wait_ge(newton_done, 4 * call + 3)
                if call >= 2:
                    dve.wait_ge(normed, BPC * (call - 1))
                dve.tensor_tensor(r, newton[:, 2, :], rstd0[:, :], ALU.mult).then_inc(newton_done, 1)
                dve.wait_ge(newton_done, 4 * call + 4)
                dve.scalar_tensor_tensor(out=neg_mean[:, call % 2, :], in0=moments[:, :, 0], scalar=-1.0, in1=r,
                                         op0=ALU.mult, op1=ALU.mult).then_inc(factors_done, 1)

            def merge(ht, p):
                dve.wait_ge(lora_done, 3 * ht + p + 1)
                dve.wait_ge(ffn_loaded[p], 16 * (ht + 1))
                if not (isinstance(ht, int) and ht == 0):
                    wait_fw_split(dve, ht - 1, p)
                dve.scalar_tensor_tensor(out=merged[:, p, :], in0=adapter_bank(ht)[:, :], scalar=LORA_SCALE,
                                         in1=ffn_raw[:, p, :], op0=ALU.mult, op1=ALU.add).then_inc(merge_done, 1)

            def split_fw(ht, p):
                if isinstance(ht, int) and ht == HT - 1:
                    dve.wait_ge(last_hi_done, p + 1)
                    low(last_lo[:, p, :], merged[:, p, :], last_hi[:, p, :].bitcast(f32), last_split)
                    return
                dve.wait_ge(fw_hi_done, 3 * ht + p + 1)
                low(fw_lo[:, p, :], merged[:, p, :], fw_hi[:, p, :].bitcast(f32), fw_split)

            def lora_kept_low():
                lo = slice(P // 2, P)
                dve.wait_ge(lora_kept_hi_done, 2)
                low(a_stack[lo, :, :], a_raw[lo, :, :], a_stack[lo, :, :].bitcast(f32), lora_kept_split)
                lo = slice(2 * SECTION, 3 * SECTION)
                low(b2_stack[lo, :], b2_raw[lo, :], b2_stack[lo, :].bitcast(f32), lora_kept_split)

            def lora_low(ht):
                dve.wait_ge(lora_hi_done, 2 * (ht + 1))
                low(b_lo[:, :, :], b_raw[0:P // 2, :, :], b_hi[0:P // 2, :, :].bitcast(f32), lora_split)
                lo = slice(SECTION, 2 * SECTION)
                low(a2_stack[lo, :], a2_raw[lo, :], a2_stack[lo, :].bitcast(f32), lora_split)

            def split_y(blocks):
                for b in blocks:
                    dve.wait_ge(y_hi_done, b + 1)
                    hi, lo = normed_columns(b // BPC)
                    cols = slice(b % BPC * P, (b % BPC + 1) * P)
                    low(lo[:, :, cols], turn_bank(b)[:, :].rearrange("p (k t) -> p k t", k=KD), hi[:, :, cols].bitcast(f32), y_split)

            def make_gate(step):
                dve.wait_ge(silu_done, step + 1)
                dve.wait_ge(h3_done, step + 1)
                if not (isinstance(step, int) and step == 0):
                    dve.wait_ge(g_split, step)
                dve.tensor_tensor(gate[:, :], ps_h3[:, :], silu[:, :], ALU.mult).then_inc(gate_done, 1)

            def add_ffn(step, m, t):
                dve.wait_ge(down_done, BPC * step + t + 1)
                b = BPC * m + t
                dve.tensor_tensor(rows[:, b, :], down_banks[t], rows[:, b, :], ALU.add).then_inc(ffn_added, 1)

            def split_g(step, parity):
                dve.wait_ge(g_hi_done, step + 1)
                low(g_lo[:, parity, :], gate[:, :], g_hi[:, parity, :].bitcast(f32), g_split)

            dve.memset(none_before[:, :], NEG).then_inc(const_set, 1)
            first_w(0)
            for k in range(KD):
                split_x(0, k)
            for p in range(1, RING):
                first_w(p)
            dve.wait_ge(rope_loaded[0], 16)
            dve.wait_ge(const_set, 2)
            for p in range(ROPES):
                by_cos_(0, p, 0)
                if p == 2:
                    first_w(RING)
                if p > 2:
                    split_x(1, 2 * p - 6)
                    split_x(1, 2 * p - 5)
                rotate(0, p, 0)
            dve.wait_ge(rope_loaded[1], 16)

            def body(I, batch, first, last):
                for j in range(BLOCKS):
                    n = BLOCKS * I + j
                    C = next_chunk(I, j)
                    parity = (j // BPC + 1) % 2
                    early, late = EARLY[j % BPC], late_done(j)
                    projects = not (last and j >= BPC)
                    rotates_late = projects and late not in (None, V_PROJ)
                    if not (first and j == 0):
                        split_pt(n - 1)
                    if projects:
                        by_cos_(C, early, parity)
                    row_max(n, j)
                    if not projects:
                        split_y(TAIL_TURNS[j, 0])
                        if j - 1 in TAIL_ADAPTERS:
                            split_fw(0, TAIL_ADAPTERS[j - 1])
                    if isinstance(I, int) and (I, j) in FACTORS_AT:
                        variances(FACTORS_AT[I, j])
                    normalise(n)
                    if not (first and j < 2):
                        before = j < 2 and isinstance(I, int) and I == KV_HEADS
                        if isinstance(I, int) and I == KV_HEADS * batch and j == 2:
                            dve.wait_ge(rows_loaded[batch], 16)
                        add_rows(n - 2, BLOCKS * (batch - before) + (j - 2) % BLOCKS)
                    if not projects and j in TAIL_ADAPTERS:
                        merge(0, TAIL_ADAPTERS[j])
                    if isinstance(I, int) and (I, j) in FACTORS_AT:
                        factors(FACTORS_AT[I, j])
                    if projects:
                        rotate(C, early, parity)
                    if j % BPC == 0:
                        split_v(2 * I + j // BPC, j // BPC)
                    if rotates_late:
                        by_cos_(C, late, parity)
                    if not projects:
                        split_y(TAIL_TURNS[j, 1])
                    if not (first and j == 0):
                        split_o(n - 1)
                    if last and j == BPC:
                        lora_kept_low()
                        lora_low(0)
                    for p in SPLITS.get(j, []):
                        if not (last and p >= WO_PIECES):
                            split_w(I, p)
                    if rotates_late:
                        rotate(C, late, parity)
                    for call, t in STATS_AT.get((I, j), []) if isinstance(I, int) else []:
                        row_stats(call, t)
                    if isinstance(I, int) and I == KV_HEADS - 1 and j % BPC < 2:
                        for k in range(KD // 2 * (j % BPC), KD // 2 * (j % BPC + 1)):
                            split_x(2 + j // BPC, k)
            iterations(dve, body)
            n = BLOCKS * ITERS
            split_pt(n - 1)
            split_fw(0, 2)
            lora_low(1)
            add_rows(n - 2, ALL_BLOCKS - 2)
            split_o(n - 1)
            make_gate(0)
            add_rows(n - 1, ALL_BLOCKS - 1)

            row_stats(CHUNKS - 1, 2)
            row_stats(CHUNKS - 1, 3)
            variances(CHUNKS - 1)

            def ffn_body(ht, first):
                for m in range(CHUNKS):
                    step = CHUNKS * ht + m
                    split_y(FFN_TURNS.get((m, 0), []) if first else [])
                    if m == CHUNKS - 1:
                        split_fw(ht + 1, 0)
                    if not (first and m == 0):
                        make_gate(step)
                    split_y(FFN_TURNS.get((m, 1), []) if first else [])
                    if first and m == 0:
                        split_y(FFN_TURNS[0, 2])
                        factors(CHUNKS - 1)
                    else:
                        for t in range(BPC):
                            add_ffn(step - 1, (m - 1) % CHUNKS, t)
                    split_g(step, m % 2)
                    split_y(FFN_TURNS.get((m, 2), []) if first and m else [])
                    if m:
                        merge(ht + 1, m - 1)
                    if m == CHUNKS - 1:
                        split_fw(ht + 1, 1)
                    if not first and m == 0:
                        lora_low(ht + 1)
                        split_fw(ht, 2)
            hidden_tiles(dve, ffn_body)

            lora_low(HT - 1)
            for m, u in pair_steps:
                step = PAIR_STEP + 2 * m + u
                if step == PAIR_STEP:
                    merge(HT - 1, 0)
                    split_fw(HT - 1, 0)
                if step == PAIR_STEP + 1:
                    merge(HT - 1, 2)
                make_gate(step)
                if step == PAIR_STEP:
                    merge(HT - 1, 1)
                if u == 0:
                    for t in range(BPC):
                        add_ffn(step - 1, (m - 1) % CHUNKS, t)
                split_g(step, u)
                if step == PAIR_STEP:
                    split_fw(HT - 1, 1)
                    split_fw(HT - 2, 2)
                if step == PAIR_STEP + 1:
                    split_fw(HT - 1, 2)
                if m and u == 0:
                    for t in range(BPC):
                        row_stats(CHUNKS + m - 1, t)
                    variances(CHUNKS + m - 1)
                if m and u:
                    factors(CHUNKS + m - 1)
            last_call = 2 * CHUNKS - 1
            add_ffn(step, CHUNKS - 1, 0)
            for t in range(1, BPC):
                add_ffn(step, CHUNKS - 1, t)
                row_stats(last_call, t - 1)
            row_stats(last_call, BPC - 1)
            variances(last_call)
            factors(last_call)
            for t in range(BPC // 2, BPC):
                b = ALL_BLOCKS - BPC + t
                dve.tensor_scalar(rows[:, b, :], rows[:, b, :], moments[:, t, 0:1], rstd[:, last_call % 2, t:t + 1],
                                  ALU.subtract, ALU.mult).then_inc(last_normed, 1)


def _tables():
    half = HEAD // 2
    inv = np.power(np.float32(THETA), -np.arange(half, dtype=np.float32) / np.float32(half)).astype(np.float32)
    angle = np.arange(SEQ, dtype=np.float32)[None, :] * inv[:, None]
    cos, sin = np.cos(angle).astype(np.float32), np.sin(angle).astype(np.float32)
    rope = np.stack([np.concatenate([cos, cos]), np.concatenate([-sin, sin])], axis=1)
    sub, slot, query = np.arange(SUBS)[None, :, None], np.arange(P)[None, None, :], (np.arange(P) % SUB)[:, None, None]
    outside = slot > sub * SUB + query
    key = np.arange(SUB)[None, None, :]
    merging = np.concatenate([key <= query, key > query], axis=1)
    return np.ascontiguousarray(rope), outside.astype(np.int32), merging.astype(np.int32), np.eye(P, dtype=np.float32)


def kernel(L0_attn_x, L0_attn_wq, L0_attn_wk, L0_attn_wv, L0_attn_wo, L0_ffn_w1, L0_ffn_w3, L0_ffn_w2,
           L0_ffn_lora_A1, L0_ffn_lora_B1, L0_ffn_lora_A3, L0_ffn_lora_B3, L0_ffn_lora_A2, L0_ffn_lora_B2):
    from concourse import bacc
    from concourse.bass_utils import run_bass_kernel_spmd

    x, wq, wk, wv, wo, w1, w3, w2, a1, b1, a3, b3, a2, b2 = (np.asarray(a) for a in (
        L0_attn_x, L0_attn_wq, L0_attn_wk, L0_attn_wv, L0_attn_wo, L0_ffn_w1, L0_ffn_w3, L0_ffn_w2,
        L0_ffn_lora_A1, L0_ffn_lora_B1, L0_ffn_lora_A3, L0_ffn_lora_B3, L0_ffn_lora_A2, L0_ffn_lora_B2))
    f = x.dtype
    rope, outside, merging, ident = _tables()

    x_rows = x.reshape(ALL_BLOCKS, P, DIM).transpose(1, 0, 2)
    x_cols = x.reshape(CHUNKS, CHUNK, KD, P).transpose(0, 3, 2, 1)
    q_pieces = wq.reshape(KD, P, KV_HEADS, GROUP, HEAD).transpose(2, 3, 1, 0, 4)
    k_pieces = wk.reshape(KD, P, KV_HEADS, 1, HEAD).transpose(2, 3, 1, 0, 4)
    v_pieces = wv.reshape(KD, P, KV_HEADS, 1, HEAD).transpose(2, 3, 1, 0, 4)
    qkv = np.concatenate([q_pieces, k_pieces, v_pieces], axis=1).reshape(KV_HEADS, PROJ, P, CHUNK)
    wo_pieces = wo.reshape(KV_HEADS, GROUP, P, DIM)
    attn_w = np.concatenate([wo_pieces, np.roll(qkv, -1, axis=0)], axis=1).reshape(-1, P, CHUNK)
    pad = HT * P - HIDDEN

    def up_tiles(w):
        w = np.pad(w, ((0, pad), (0, 0)))
        return w.reshape(HT, P, KD, P).transpose(0, 3, 2, 1).reshape(HT, P, CHUNK)

    def hidden_tiles(w):
        return np.pad(w, ((0, pad), (0, 0))).reshape(HT, P, -1)

    ffn_w = np.stack([up_tiles(w1), up_tiles(w3), hidden_tiles(w2.T)], axis=1).reshape(-1, P, CHUNK)
    lora_a = np.stack([a.reshape(RANK, KD, P).transpose(1, 0, 2).reshape(KD * RANK, P) for a in (a1, a3)], axis=1)
    lora_a = np.concatenate([lora_a, lora_a], axis=0)
    lora_b = np.zeros((HT, 2, KD, RANK, 2, KD, P), f)
    for p, b in enumerate((b1, b3)):
        for k in range(KD):
            lora_b[:, :, k, :, p, k, :] = hidden_tiles(b).transpose(0, 2, 1)[:, None]
    lora_b = lora_b.reshape(HT, P, 2, CHUNK)
    lora_a2 = np.zeros((HT, 3, SECTION, P), f)
    lora_a2[:, :, :RANK, :] = hidden_tiles(a2.T).transpose(0, 2, 1)[:, None]
    lora_a2 = lora_a2.reshape(HT, 3 * SECTION, P)
    lora_b2 = np.zeros((3, SECTION, DIM), f)
    lora_b2[:, :RANK, :] = b2.T
    lora_b2 = lora_b2.reshape(3 * SECTION, DIM)

    arrays = {"x_rows": x_rows, "x_cols": x_cols, "attn_w": attn_w, "rope": rope, "outside": outside, "merging": merging, "ident": ident,
              "ffn_w": ffn_w, "lora_a": lora_a, "lora_b": lora_b, "lora_a2": lora_a2, "lora_b2": lora_b2}
    arrays = {k: np.ascontiguousarray(v) for k, v in arrays.items()}
    nc = bacc.Bacc("TRN2", target_bir_lowering=False, num_devices=1)
    args = [nc.dram_tensor(k, v.shape, mybir.dt.from_np(v.dtype), kind="ExternalInput").ap() for k, v in arrays.items()]
    out = nc.dram_tensor("out", (P, ALL_BLOCKS, DIM), mybir.dt.from_np(np.dtype(f)), kind="ExternalOutput").ap()
    attention_and_ffn(nc, *args, out)
    got = run_bass_kernel_spmd(nc, [arrays], core_ids=[0]).results[0]["out"]
    return np.asarray(got).transpose(1, 0, 2).reshape(BATCH, SEQ, DIM)
```
